# Optimizing a Trainium2 kernel written in Bass

```python
import numpy as np
import jax
import jax.numpy as jnp

def _softmax(x, axis=-1):
    return jax.nn.softmax(x, axis=axis)

def _gelu(x):
    return jax.nn.gelu(x, approximate=True)

def _silu(x):
    return jax.nn.silu(x)

def _sigmoid(x):
    return jax.nn.sigmoid(x)

def _layernorm(x, axis=-1, eps=1e-05):
    m = jnp.mean(x, axis=axis, keepdims=True)
    v = jnp.var(x, axis=axis, keepdims=True)
    return (x - m) / jnp.sqrt(v + eps)

def _scatter_add(tgt, idx, src, axis=0):
    return tgt.at[idx].add(src)

def _segment_sum(src, seg, n):
    return jax.ops.segment_sum(src, seg, n)
kernel_name = 'mk_seq_postln_d1_jaxref_r4_035990'

def setup_inputs(seed: int=0):
    np.random.seed(seed)
    _w = jnp.asarray

    def _L0_attn_setup():
        import jax, jax.numpy as jnp
        import numpy as np
        TAU_INV = 0.5
        V_TH = 1.0
        DECAY = 0.9
        ATAN_ALPHA = 2.0
        LN_EPS = 1e-05

        @jax.custom_vjp
        def spike(x):
            return (x >= 0.0).astype(x.dtype)

        def _spike_fwd(x):
            return (spike(x), x)

        def _spike_bwd(x, g):
            sg = ATAN_ALPHA * 0.5 / (1.0 + (jnp.pi * 0.5 * ATAN_ALPHA * x) ** 2)
            return (g * sg,)
        spike.defvjp(_spike_fwd, _spike_bwd)

        def lif_step(v, x_t):
            v = v + (x_t - v) * TAU_INV
            s = spike(v - V_TH)
            v = v * (1.0 - s)
            return (v, s)

        def lif_scan(x):
            xT = jnp.swapaxes(x, 0, 1)
            _, sT = jax.lax.scan(lif_step, jnp.zeros_like(xT[0]), xT)
            return jnp.swapaxes(sT, 0, 1)

        def layernorm(x, g, b):
            mu = jnp.mean(x, axis=-1, keepdims=True)
            var = jnp.mean((x - mu) ** 2, axis=-1, keepdims=True)
            return (x - mu) * jax.lax.rsqrt(var + LN_EPS) * g + b

        def srwkv_forward(x, Wr, Wk, Wv, Wo, W1, b1, W2, b2, ln1_g, ln1_b, ln2_g, ln2_b):
            residual = x
            R = jnp.einsum('btd,ed->bte', x, Wr)
            K = jnp.einsum('btd,ed->bte', x, Wk)
            V = jnp.einsum('btd,ed->bte', x, Wv)
            RT = jnp.swapaxes(R, 0, 1)
            KT = jnp.swapaxes(K, 0, 1)
            VT = jnp.swapaxes(V, 0, 1)
            B, _, D = x.shape
            z = jnp.zeros((B, D), dtype=x.dtype)

            def step(carry, inp):
                h, vr, vk, vv = carry
                r_in, k_in, v_in = inp
                vr, r = lif_step(vr, r_in)
                vk, k = lif_step(vk, k_in)
                vv, v = lif_step(vv, v_in)
                h = h * DECAY + k * v
                y = r * h
                return ((h, vr, vk, vv), y)
            _, yT = jax.lax.scan(step, (z, z, z, z), (RT, KT, VT))
            attn_out = jnp.einsum('tbd,ed->bte', yT, Wo)
            x1 = layernorm(residual + attn_out, ln1_g, ln1_b)
            h1 = jnp.einsum('btd,fd->btf', x1, W1) + b1
            s1 = lif_scan(h1)
            h2 = jnp.einsum('btf,df->btd', s1, W2) + b2
            ffn_out = lif_scan(h2)
            return layernorm(x1 + ffn_out, ln2_g, ln2_b)
        key = jax.random.key(seed)
        ks = jax.random.split(key, 8)
        B, T, D, F = (8, 256, 256, 1024)
        s_d = 1.0 / np.sqrt(D)
        s_f = 1.0 / np.sqrt(F)
        return {'x': jax.random.normal(ks[0], (B, T, D), jnp.float32), 'Wr': jax.random.normal(ks[1], (D, D), jnp.float32) * s_d, 'Wk': jax.random.normal(ks[2], (D, D), jnp.float32) * s_d, 'Wv': jax.random.normal(ks[3], (D, D), jnp.float32) * s_d, 'Wo': jax.random.normal(ks[4], (D, D), jnp.float32) * s_d, 'W1': jax.random.normal(ks[5], (F, D), jnp.float32) * s_d, 'b1': jnp.zeros((F,), jnp.float32), 'W2': jax.random.normal(ks[6], (D, F), jnp.float32) * s_f, 'b2': jnp.zeros((D,), jnp.float32), 'ln1_g': jnp.ones((D,), jnp.float32), 'ln1_b': jnp.zeros((D,), jnp.float32), 'ln2_g': jnp.ones((D,), jnp.float32), 'ln2_b': jnp.zeros((D,), jnp.float32)}
    _L0_attn_in = _L0_attn_setup()

    def _L0_ffn_setup():
        import jax, jax.numpy as jnp
        import numpy as np
        B, S, D = (4, 512, 256)
        O = 256
        E = 8
        K = 2
        key = jax.random.key(seed)
        k1, k2, k3, k4, k5 = jax.random.split(key, 5)
        scale = 1.0 / np.sqrt(D)
        x = jax.random.normal(k1, (B, S, D), dtype=jnp.float32)
        We = jax.random.uniform(k2, (E, D, O), dtype=jnp.float32, minval=-scale, maxval=scale)
        be = jax.random.uniform(k3, (E, O), dtype=jnp.float32, minval=-scale, maxval=scale)
        Wg = jax.random.uniform(k4, (D, E), dtype=jnp.float32, minval=-scale, maxval=scale)
        bg = jax.random.uniform(k5, (E,), dtype=jnp.float32, minval=-scale, maxval=scale)
        return {'x': x, 'We': We, 'be': be, 'Wg': Wg, 'bg': bg}
    _L0_ffn_in = _L0_ffn_setup()
    _d = {'L0_attn_x': _L0_attn_in['x'], 'L0_attn_Wr': _L0_attn_in['Wr'], 'L0_attn_Wk': _L0_attn_in['Wk'], 'L0_attn_Wv': _L0_attn_in['Wv'], 'L0_attn_Wo': _L0_attn_in['Wo'], 'L0_attn_W1': _L0_attn_in['W1'], 'L0_attn_b1': _L0_attn_in['b1'], 'L0_attn_W2': _L0_attn_in['W2'], 'L0_attn_b2': _L0_attn_in['b2'], 'L0_attn_ln1_g': _L0_attn_in['ln1_g'], 'L0_attn_ln1_b': _L0_attn_in['ln1_b'], 'L0_attn_ln2_g': _L0_attn_in['ln2_g'], 'L0_attn_ln2_b': _L0_attn_in['ln2_b'], 'L0_ffn_We': _L0_ffn_in['We'], 'L0_ffn_be': _L0_ffn_in['be'], 'L0_ffn_Wg': _L0_ffn_in['Wg'], 'L0_ffn_bg': _L0_ffn_in['bg']}
    _x0 = _d['L0_attn_x']
    _d['L0_attn_x'] = jax.random.normal(jax.random.fold_in(jax.random.key(seed), 1), (16, 512, 256), dtype=_x0.dtype)
    del _x0
    return _d

def reference(L0_attn_x, L0_attn_Wr, L0_attn_Wk, L0_attn_Wv, L0_attn_Wo, L0_attn_W1, L0_attn_b1, L0_attn_W2, L0_attn_b2, L0_attn_ln1_g, L0_attn_ln1_b, L0_attn_ln2_g, L0_attn_ln2_b, L0_ffn_We, L0_ffn_be, L0_ffn_Wg, L0_ffn_bg):

    def _L0_attn_ref(x, Wr, Wk, Wv, Wo, W1, b1, W2, b2, ln1_g, ln1_b, ln2_g, ln2_b):
        import jax, jax.numpy as jnp
        import numpy as np
        TAU_INV = 0.5
        V_TH = 1.0
        DECAY = 0.9
        ATAN_ALPHA = 2.0
        LN_EPS = 1e-05

        @jax.custom_vjp
        def spike(x):
            return (x >= 0.0).astype(x.dtype)

        def _spike_fwd(x):
            return (spike(x), x)

        def _spike_bwd(x, g):
            sg = ATAN_ALPHA * 0.5 / (1.0 + (jnp.pi * 0.5 * ATAN_ALPHA * x) ** 2)
            return (g * sg,)
        spike.defvjp(_spike_fwd, _spike_bwd)

        def lif_step(v, x_t):
            v = v + (x_t - v) * TAU_INV
            s = spike(v - V_TH)
            v = v * (1.0 - s)
            return (v, s)

        def lif_scan(x):
            xT = jnp.swapaxes(x, 0, 1)
            _, sT = jax.lax.scan(lif_step, jnp.zeros_like(xT[0]), xT)
            return jnp.swapaxes(sT, 0, 1)

        def layernorm(x, g, b):
            mu = jnp.mean(x, axis=-1, keepdims=True)
            var = jnp.mean((x - mu) ** 2, axis=-1, keepdims=True)
            return (x - mu) * jax.lax.rsqrt(var + LN_EPS) * g + b

        def srwkv_forward(x, Wr, Wk, Wv, Wo, W1, b1, W2, b2, ln1_g, ln1_b, ln2_g, ln2_b):
            residual = x
            R = jnp.einsum('btd,ed->bte', x, Wr)
            K = jnp.einsum('btd,ed->bte', x, Wk)
            V = jnp.einsum('btd,ed->bte', x, Wv)
            RT = jnp.swapaxes(R, 0, 1)
            KT = jnp.swapaxes(K, 0, 1)
            VT = jnp.swapaxes(V, 0, 1)
            B, _, D = x.shape
            z = jnp.zeros((B, D), dtype=x.dtype)

            def step(carry, inp):
                h, vr, vk, vv = carry
                r_in, k_in, v_in = inp
                vr, r = lif_step(vr, r_in)
                vk, k = lif_step(vk, k_in)
                vv, v = lif_step(vv, v_in)
                h = h * DECAY + k * v
                y = r * h
                return ((h, vr, vk, vv), y)
            _, yT = jax.lax.scan(step, (z, z, z, z), (RT, KT, VT))
            attn_out = jnp.einsum('tbd,ed->bte', yT, Wo)
            x1 = layernorm(residual + attn_out, ln1_g, ln1_b)
            h1 = jnp.einsum('btd,fd->btf', x1, W1) + b1
            s1 = lif_scan(h1)
            h2 = jnp.einsum('btf,df->btd', s1, W2) + b2
            ffn_out = lif_scan(h2)
            return layernorm(x1 + ffn_out, ln2_g, ln2_b)
        return srwkv_forward(x, Wr, Wk, Wv, Wo, W1, b1, W2, b2, ln1_g, ln1_b, ln2_g, ln2_b)

    def _L0_ffn_ref(x, We, be, Wg, bg):
        import jax, jax.numpy as jnp
        import numpy as np
        B, S, D = (4, 512, 256)
        O = 256
        E = 8
        K = 2
        b, s, d = x.shape
        x_flat = x.reshape(-1, d)
        gates = jax.nn.softmax(x_flat @ Wg + bg, axis=-1)
        topk_gates, topk_idx = jax.lax.top_k(gates, K)
        topk_gates = topk_gates / jnp.sum(topk_gates, axis=1, keepdims=True)
        expert_out = jnp.einsum('nd,edo->neo', x_flat, We) + be
        selected = jnp.take_along_axis(expert_out, topk_idx[:, :, None], axis=1)
        out = jnp.sum(selected * topk_gates[:, :, None], axis=1)
        return out.reshape(b, s, -1)
    x = L0_attn_x
    x = _layernorm(x + _L0_attn_ref(x, L0_attn_Wr, L0_attn_Wk, L0_attn_Wv, L0_attn_Wo, L0_attn_W1, L0_attn_b1, L0_attn_W2, L0_attn_b2, L0_attn_ln1_g, L0_attn_ln1_b, L0_attn_ln2_g, L0_attn_ln2_b), axis=-1)
    x = _layernorm(x + _L0_ffn_ref(x, L0_ffn_We, L0_ffn_be, L0_ffn_Wg, L0_ffn_bg), axis=-1)
    return x

_drawn_inputs = setup_inputs


def setup_inputs(seed=0):
    import zlib

    import numpy as np

    out = dict(_drawn_inputs(seed))
    spreads = {'L0_attn_b1': (0.0, 0.1),
     'L0_attn_b2': (0.0, 0.1),
     'L0_attn_ln1_g': (1.0, 0.2),
     'L0_attn_ln1_b': (0.0, 0.1),
     'L0_attn_ln2_g': (1.0, 0.2),
     'L0_attn_ln2_b': (0.0, 0.1)}
    factors = {'L0_attn_Wr': 3.425, 'L0_attn_Wk': 3.647, 'L0_attn_Wv': 3.328, 'L0_attn_Wo': 3.92}
    for name, (base, spread) in spreads.items():
        noise = np.random.default_rng([zlib.crc32(name.encode()), seed]).standard_normal(out[name].shape)
        drawn = base * np.exp(spread * noise) if base else spread * noise
        out[name] = jnp.asarray(drawn.astype(out[name].dtype))
    for name, factor in factors.items():
        out[name] = (out[name] * factor).astype(out[name].dtype)
    return out
```

```python
from contextlib import ExitStack

import concourse.bass as bass
from concourse import mybir

F32 = mybir.dt.float32
F32R = mybir.dt.float32r
U32 = mybir.dt.uint32
ALU = mybir.AluOpType
ACT = mybir.ActivationFunctionType

P = 128
B, T, D, F, E = 16, 512, 256, 1024, 8
STEPS = 16
N = STEPS * B
CHUNKS = T // STEPS
TILES = N // P
DK = D // P
FK = F // P
RKV_TILES = 3 * DK
EPS = 1e-5
THRESHOLD = 2.0
DECAY = 0.9

COL_H1 = RKV_TILES * B
COL_H2 = COL_H1 + FK * B
COLS = COL_H2 + DK * B

LAG_RKV = -1
LAG_Y = 1
LAG_S = 3
LAG_Z = 5
LAG_M = 6
LAG_F = 7
LIF_BEATS = CHUNKS + 4
FIRST_STEADY = LAG_F
UNROLL = 4
STEADY_TURNS = (CHUNKS - 1 + LAG_RKV + 1 - FIRST_STEADY) // UNROLL
FIRST_DRAIN = FIRST_STEADY + UNROLL * STEADY_TURNS
LAST_BEAT = CHUNKS - 1 + LAG_F

C_B1, C_B2, C_G1, C_BE1 = 0, FK, FK + DK, FK + 2 * DK
C_BG = C_BE1 + DK
C_IOTA = C_BG + TILES * E
C_ID = C_IOTA + E
C_G2 = C_ID + P
C_BE2 = C_G2 + D
C_BEXP = C_BE2 + D
C_ALL = C_BEXP + D

PIECE = DK * D
PIECE0 = DK * (D + E)
W1_PIECES = DK * F // PIECE
W2_PIECES = FK * D // PIECE
PIECES = W1_PIECES + W2_PIECES + E
RAW_SLOTS = 4


class Beat:

    def __init__(self, k, turn=None):
        self.k, self.turn = k, turn

    def value(self, per, lag, add=0):
        n = per * (self.k - lag) + add
        return n if self.turn is None else self.turn * (UNROLL * per) + n

    def has(self, lag):
        return self.turn is not None or 0 <= self.k - lag < CHUNKS

    def lif(self):
        return self.turn is not None or 0 <= self.k < LIF_BEATS

    def chunk(self, lag):
        return self.value(1, lag)

    def slot(self, lag, slots):
        return (self.k - lag) % slots

    def fills(self, add=0):
        if self.turn is not None:
            return self.turn * (UNROLL * 8) + 8 * self.k - 4 + add
        done = lambda lag: min(max(self.k - lag, 0), CHUNKS)
        return 3 * done(LAG_RKV) + 4 * done(LAG_Y) + done(LAG_S) + add

    def loads(self, lag, slots):
        n = 16 * ((self.k - lag) // slots + 1)
        return n if self.turn is None else self.turn * (16 * UNROLL // slots) + n


def some(n):
    return not isinstance(n, int) or n > 0


def build(nc, x_T, x_tok, w_rkv, w_o, w_1, w_2, w_e0, w_e, consts, out):
    with ExitStack() as ctx:
        def sb(name, shape, dt=F32):
            return ctx.enter_context(nc.sbuf_tensor(name, shape, dt))

        def sem(name):
            return ctx.enter_context(nc.semaphore(name))

        wrkv = sb("wrkv", [P, DK, RKV_TILES * P])
        wo = sb("wo", [P, DK, D])
        w1_hi, w1_lo = sb("w1_hi", [P, DK * F], F32R), sb("w1_lo", [P, DK * F], F32R)
        w2_hi, w2_lo = sb("w2_hi", [P, FK * D], F32R), sb("w2_lo", [P, FK * D], F32R)
        we0_hi, we0_lo = sb("we0_hi", [P, PIECE0], F32R), sb("we0_lo", [P, PIECE0], F32R)
        we_hi, we_lo = sb("we_hi", [P, E - 1, PIECE], F32R), sb("we_lo", [P, E - 1, PIECE], F32R)
        cst = sb("cst", [P, C_ALL])
        ident = cst[:, C_ID:C_ID + P]
        ln2_gain = cst[:, C_G2:C_G2 + D]
        ln2_bias = cst[:, C_BE2:C_BE2 + D]
        expert_bias = cst[0:E, C_BEXP:C_BEXP + D]
        decay = sb("decay", [P, DK * B, STEPS])
        neg_half = sb("neg_half", [P, TILES])
        X = sb("X", [P, 2, STEPS, COLS])
        U = sb("U", [P, 2, STEPS, COLS])
        xt = sb("xt", [P, 2, DK, N])
        xa = sb("xa", [P, TILES, D])
        h = sb("h", [P, DK * B, STEPS])
        h_last = sb("h_last", [P, DK * B])
        y = sb("y", [P, DK * N])
        v_spikes = y[:].rearrange("p (t c) -> p t c", t=STEPS)
        x1n = sb("x1n", [P, TILES, D])
        x1 = sb("x1", [P, 4, DK, N])
        x1_hi, x1_lo = sb("x1_hi", [P, DK, N], F32R), sb("x1_lo", [P, DK, N], F32R)
        s1 = sb("s1", [P, FK, N], F32R)
        z = sb("z", [P, DK, N])
        xb = sb("xb", [P, TILES, D])
        w = sb("w", [P, TILES, D])
        x3 = sb("x3", [P, TILES, D])
        x3_hi, x3_lo = sb("x3_hi", [P, 2, DK, N], F32R), sb("x3_lo", [P, 2, DK, N], F32R)
        term = sb("term", [P, RAW_SLOTS, PIECE0])
        psum_terms = sb("psum_terms", [P, TILES, D])
        acc = sb("acc", [P, TILES, D])
        res = sb("res", [P, TILES, D])
        logit = sb("logit", [P, TILES, E])
        top = sb("top", [P, TILES, 8])
        top_at = sb("top_at", [P, TILES, 8], U32)
        top_atf = sb("top_atf", [P, TILES, 2])
        gdiff, gexp = sb("gdiff", [P, TILES]), sb("gexp", [P, TILES])
        gden, g1st, g2nd = sb("gden", [P, TILES]), sb("g1st", [P, TILES]), sb("g2nd", [P, TILES])
        gate_b = sb("gate_b", [P, TILES, E])
        gate = sb("gate", [P, 2, TILES, E])
        gate_T = sb("gate_T", [E, TILES, P])
        stats = [sb(f"stats{i}", [P, TILES, 6]) for i in range(4)]
        mv = [sb(f"mv{i}", [P, TILES, 2]) for i in range(4)]
        veps = [sb(f"veps{i}", [P, TILES]) for i in range(4)]
        rstd = [sb(f"rstd{i}", [P, TILES]) for i in range(4)]

        ps_proj = ctx.enter_context(nc.psum_tensor("ps_proj", [P, 2, 2, N], F32))
        ps_attn = ctx.enter_context(nc.psum_tensor("ps_attn", [P, 2, 256], F32))
        ps_zx = ctx.enter_context(nc.psum_tensor("ps_zx", [P, 2, 256], F32))
        ps_e0 = ctx.enter_context(nc.psum_tensor("ps_e0", [P, TILES, 512], F32))
        ps_e = ctx.enter_context(nc.psum_tensor("ps_e", [P, 2, TILES, D], F32))

        fixed_loaded = sem("fixed_loaded")
        wo_loaded = sem("wo_loaded")
        raw_loaded = [sem(f"raw_loaded{i}") for i in range(RAW_SLOTS)]
        split_hi, split_lo = sem("split_hi"), sem("split_lo")
        xt_loaded = [sem("xt_loaded0"), sem("xt_loaded1")]
        xa_loaded, xb_loaded = sem("xa_loaded"), sem("xb_loaded")
        out_stored = sem("out_stored")
        vec_set, pool_set = sem("vec_set"), sem("pool_set")
        proj_filled, proj_read = sem("proj_filled"), sem("proj_read")
        lif = sem("lif")
        y_steps, attn_done, ln1_steps = sem("y_steps"), sem("attn_done"), sem("ln1_steps")
        x1T_done, x1_ready, x1_lo_ready = sem("x1T_done"), sem("x1_ready"), sem("x1_lo_ready")
        s1_ready = sem("s1_ready")
        z_ready, zT_done, xb_ready = sem("z_ready"), sem("zT_done"), sem("xb_ready")
        ln2_steps, ln3_steps = sem("ln2_steps"), sem("ln3_steps")
        x3T_done, x3_hi_ready, x3_lo_ready = sem("x3T_done"), sem("x3_hi_ready"), sem("x3_lo_ready")
        rstd_ready = [sem(f"rstd_ready{i}") for i in range(4)]
        e0_done, expert_done = sem("e0_done"), sem("expert_done")
        gate_steps, gexp_ready = sem("gate_steps"), sem("gexp_ready")
        gateT_done, gateT_ready, bias_done = sem("gateT_done"), sem("gateT_ready"), sem("bias_done")
        e0_added, term_ready, sum_steps = sem("e0_added"), sem("term_ready"), sem("sum_steps")
        fin_steps = sem("fin_steps")
        dve_waited, pool_waited = sem("dve_waited"), sem("pool_waited")

        Y_STEPS, LN1_STEPS, LN2_STEPS, LN3_STEPS, GATE_STEPS, FIN_STEPS, SUM_STEPS = 7, 7, 8, 6, 15, 7, 7

        def pieces_of(p):
            if p < W1_PIECES:
                s = slice(p * PIECE, (p + 1) * PIECE)
                return w_1[:, s], w1_hi[:, s], w1_lo[:, s], PIECE
            p -= W1_PIECES
            if p < W2_PIECES:
                s = slice(p * PIECE, (p + 1) * PIECE)
                return w_2[:, s], w2_hi[:, s], w2_lo[:, s], PIECE
            p -= W2_PIECES
            if p == 0:
                return w_e0, we0_hi[:, :], we0_lo[:, :], PIECE0
            return w_e[p - 1], we_hi[:, p - 1, :], we_lo[:, p - 1, :], PIECE

        def pieces_in(k):
            per = {-1: range(0, 4), 0: range(4, 8), 1: range(8, 11), 2: range(11, 14), 3: range(14, 16)}
            return per.get(k, range(0))

        def run_beats(eng, beat):
            for k in range(-1, FIRST_STEADY):
                beat(Beat(k))
            with eng.Fori(0, STEADY_TURNS) as turn:
                for u in range(UNROLL):
                    beat(Beat(FIRST_STEADY + u, turn))
            for k in range(FIRST_DRAIN, LAST_BEAT + 1):
                beat(Beat(k))

        block = ctx.enter_context(nc.Block())

        @block.sync
        def _(sp):
            def load_xt(b):
                if b.turn is not None or b.k - LAG_RKV >= 2:
                    if some(Beat(b.k - 1, b.turn).fills()):
                        sp.wait_ge(proj_filled, Beat(b.k - 1, b.turn).fills())
                s = b.slot(LAG_RKV, 2)
                sp.dma_start(xt[:, s], x_T[b.chunk(LAG_RKV)]).then_inc(xt_loaded[s], 16)

            sp.dma_start(wrkv[:], w_rkv).then_inc(fixed_loaded, 16)
            sp.dma_start(cst[:], consts).then_inc(fixed_loaded, 16)
            sp.dma_start(wo[:], w_o).then_inc(wo_loaded, 16)

            def beat(b):
                if b.has(LAG_RKV):
                    load_xt(b)
                if b.turn is None:
                    for p in pieces_in(b.k):
                        src, _, _, n = pieces_of(p)
                        if some(p - RAW_SLOTS + 1):
                            sp.wait_ge(split_lo, p - RAW_SLOTS + 1)
                        sp.dma_start(term[:, p % RAW_SLOTS, 0:n], src).then_inc(raw_loaded[p % RAW_SLOTS], 16)
                if b.has(LAG_Y - 1):
                    if some(b.value(LN1_STEPS, LAG_Y, 1)):
                        sp.wait_ge(ln1_steps, b.value(LN1_STEPS, LAG_Y, 1))
                    sp.dma_start(xa[:], x_tok[b.chunk(LAG_Y - 1)]).then_inc(xa_loaded, 16)
                if b.has(LAG_Z - 1):
                    if some(b.value(LN2_STEPS, LAG_Z, LN2_STEPS)):
                        sp.wait_ge(ln2_steps, b.value(LN2_STEPS, LAG_Z, LN2_STEPS))
                    sp.dma_start(xb[:], x_tok[b.chunk(LAG_Z - 1)]).then_inc(xb_loaded, 16)
                if b.has(LAG_F):
                    sp.wait_ge(fin_steps, b.value(FIN_STEPS, LAG_F, FIN_STEPS))
                    sp.dma_start(out[b.chunk(LAG_F)], res[:]).then_inc(out_stored, 16)

            run_beats(sp, beat)
            sp.wait_ge(out_stored, 16 * CHUNKS)

        @block.tensor
        def _(pe):
            def split_product(dst, parts, k0=True, last_k=True):
                mm, n = None, 3 * len(parts)
                i = 0
                for a_hi, a_lo, b_hi, b_lo in parts:
                    for lhs, rhs in ((a_hi, b_hi), (a_lo, b_hi), (a_hi, b_lo)):
                        mm = pe.matmul(dst, lhs, rhs, start=(i == 0), stop=(i == n - 1))
                        i += 1
                return mm

            def proj_bank(b, fill):
                if some(b.fills(fill - 1)):
                    pe.wait_ge(proj_read, b.fills(fill - 1))
                base = b.fills() if b.turn is None else 0
                return (base + fill) % 2

            def rkv(b):
                pe.wait_ge(xt_loaded[b.slot(LAG_RKV, 2)], b.loads(LAG_RKV, 2))
                for f in range(3):
                    bank = proj_bank(b, f)
                    for e in range(2):
                        for k in range(DK):
                            c = (2 * f + e) * P
                            mm = pe.matmul(ps_proj[:, bank, e, :], wrkv[:, k, c:c + P],
                                           xt[:, b.slot(LAG_RKV, 2), k, :], start=(k == 0), stop=(k == DK - 1))
                    mm.then_inc(proj_filled, 1)

            def attn(b):
                pe.wait_ge(y_steps, b.value(Y_STEPS, LAG_Y, Y_STEPS))
                if some(b.value(3, LAG_Y)):
                    pe.wait_ge(x1_ready, b.value(3, LAG_Y))
                for j in range(TILES):
                    for k in range(DK):
                        mm = pe.matmul(ps_attn[:, j, :], y[:, k * N + j * P:k * N + (j + 1) * P],
                                       wo[:, k, :], start=(k == 0), stop=(k == DK - 1))
                mm.then_inc(attn_done, 1)

            def transpose4(dst, src_tile, done):
                for i in range(2):
                    for j in range(2):
                        mm = pe.transpose(dst[:, i, j * P:(j + 1) * P], src_tile(i, j), ident)
                mm.then_inc(done, 1)

            def w2(b, fill):
                bank = proj_bank(b, fill)
                pe.wait_ge(s1_ready, b.value(4, LAG_S, 4))
                for e in range(DK):
                    for ft in range(FK):
                        for part, wp in enumerate((w2_hi, w2_lo)):
                            c = ft * D + e * P
                            mm = pe.matmul(ps_proj[:, bank, e, :], wp[:, c:c + P], s1[:, ft, :],
                                           start=(ft == 0 and part == 0), stop=(ft == FK - 1 and part == 1))
                mm.then_inc(proj_filled, 1)

            def w1(b, fill0):
                pe.wait_ge(x1_lo_ready, b.value(1, LAG_Y, 1))
                for f in range(4):
                    bank = proj_bank(b, fill0 + f)
                    for e in range(2):
                        def cols(k):
                            c = k * F + (2 * f + e) * P
                            return slice(c, c + P)
                        mm = split_product(ps_proj[:, bank, e, :],
                                           [(w1_hi[:, cols(k)], w1_lo[:, cols(k)], x1_hi[:, k, :], x1_lo[:, k, :])
                                            for k in range(DK)])
                    mm.then_inc(proj_filled, 1)

            def x3_tile(b, lag, k, j):
                s = b.slot(lag, 2)
                return x3_hi[:, s, k, j * P:(j + 1) * P], x3_lo[:, s, k, j * P:(j + 1) * P]

            def expert0(b):
                pe.wait_ge(x3_lo_ready, b.value(1, LAG_M, 1))
                if some(b.value(2, LAG_M)):
                    pe.wait_ge(e0_added, b.value(2, LAG_M))
                for j in range(TILES):
                    mm = split_product(ps_e0[:, j, 0:D + E],
                                       [(*x3_tile(b, LAG_M, k, j), we0_hi[:, k * (D + E):(k + 1) * (D + E)],
                                         we0_lo[:, k * (D + E):(k + 1) * (D + E)]) for k in range(DK)])
                mm.then_inc(e0_done, 1)

            def expert(b, e):
                if some(b.value(E - 1, LAG_M, e - 2)):
                    pe.wait_ge(term_ready, b.value(E - 1, LAG_M, e - 2))
                bank = (b.slot(LAG_M, 2) * (E - 1) + e - 1) % 2
                for j in range(TILES):
                    mm = split_product(ps_e[:, bank, j, :],
                                       [(*x3_tile(b, LAG_M, k, j), we_hi[:, e - 1, k * D:(k + 1) * D],
                                         we_lo[:, e - 1, k * D:(k + 1) * D]) for k in range(DK)])
                mm.then_inc(expert_done, 1)

            def gates_T(b):
                pe.wait_ge(gate_steps, b.value(GATE_STEPS, LAG_M, GATE_STEPS))
                if b.has(LAG_Z):
                    pe.wait_ge(x3_lo_ready, b.value(1, LAG_Z, 1))
                for j in range(TILES):
                    mm = pe.transpose(ps_zx[0:E, j, 0:P], gate[:, b.slot(LAG_M, 2), j, :], ident)
                mm.then_inc(gateT_done, 1)

            def biases(b):
                pe.wait_ge(gateT_ready, b.value(1, LAG_M, 1))
                for j in range(TILES):
                    mm = pe.matmul(ps_zx[:, j, :], gate_T[:, j, :], expert_bias, start=True, stop=True)
                mm.then_inc(bias_done, 1)

            def beat(b):
                if b.has(LAG_M):
                    if b.turn is None and b.k == LAG_M:
                        pe.wait_ge(split_lo, PIECES)
                    expert0(b)
                if b.has(LAG_Y):
                    if b.turn is None and b.k == LAG_Y:
                        pe.wait_ge(wo_loaded, 16)
                        pe.wait_ge(split_lo, W1_PIECES)
                    attn(b)
                if b.has(LAG_Z):
                    pe.wait_ge(z_ready, b.value(2, LAG_Z, 2))
                    if b.has(LAG_F):
                        pe.wait_ge(fin_steps, b.value(FIN_STEPS, LAG_F, 1))
                    transpose4(ps_zx, lambda j, k: z[:, k, j * P:(j + 1) * P], zT_done)
                fill = 0
                if b.has(LAG_RKV):
                    rkv(b)
                    fill += 3
                if b.has(LAG_S):
                    if b.turn is None and b.k == LAG_S:
                        pe.wait_ge(split_lo, W1_PIECES + W2_PIECES)
                    w2(b, fill)
                    fill += 1
                if b.has(LAG_Y):
                    pe.wait_ge(ln1_steps, b.value(LN1_STEPS, LAG_Y, LN1_STEPS))
                    transpose4(ps_attn, lambda k, j: x1n[:, j, k * P:(k + 1) * P], x1T_done)
                if b.has(LAG_M):
                    expert(b, 1)
                    expert(b, 2)
                if b.has(LAG_Y):
                    w1(b, fill)
                if b.has(LAG_Z):
                    pe.wait_ge(ln3_steps, b.value(LN3_STEPS, LAG_Z, LN3_STEPS))
                    transpose4(ps_zx, lambda k, j: x3[:, j, k * P:(k + 1) * P], x3T_done)
                if b.has(LAG_M):
                    expert(b, 3)
                    gates_T(b)
                    expert(b, 4)
                    biases(b)
                    for e in range(5, E):
                        expert(b, e)

            pe.wait_ge(fixed_loaded, 32)
            run_beats(pe, beat)

        @block.scalar
        def _(act):
            def copy(out_, in_):
                return nc.scalar.activation(out_, in_, ACT.Identity)

            def to_lif(b, fill, col, tiles, bias):
                base = b.fills() if b.turn is None else 0
                bank = (base + fill) % 2
                dst = X[:, (b.k + 1) % 2, :, :]
                act.wait_ge(proj_filled, b.fills(fill + 1))
                if bias is None:
                    v = dst[:, :, col:col + tiles * B].rearrange("p t (g b) -> p g t b", b=B)
                    copy(v, ps_proj[:, bank, 0:tiles, :].rearrange("p g (t b) -> p g t b", b=B)).then_inc(proj_read, 1)
                    return
                for e in range(tiles):
                    last = nc.scalar.activation(dst[:, :, col + e * B:col + (e + 1) * B],
                                                ps_proj[:, bank, e, :].rearrange("p (t b) -> p t b", b=B),
                                                ACT.Identity, bias=cst[:, bias + e:bias + e + 1])
                last.then_inc(proj_read, 1)

            def read_x1(b):
                slot = b.slot(LAG_Y, 4)
                act.wait_ge(x1T_done, b.value(1, LAG_Y, 1))
                if some(b.value(2, LAG_Y + 4, 2)):
                    act.wait_ge(z_ready, b.value(2, LAG_Y + 4, 2))
                if some(b.fills()):
                    act.wait_ge(proj_filled, b.fills())
                for k in range(DK):
                    nc.scalar.activation(x1[:, slot, k, :], ps_attn[:, k, :], ACT.Identity,
                                         bias=cst[:, C_BE1 + k:C_BE1 + k + 1],
                                         scale=cst[:, C_G1 + k:C_G1 + k + 1]).then_inc(x1_ready, 1)
                act.wait_ge(x1_ready, b.value(3, LAG_Y, 2))
                copy(x1_hi[:], x1[:, slot]).then_inc(x1_ready, 1)

            def read_expert(b, e):
                slot = (e - 1) % RAW_SLOTS
                act.wait_ge(expert_done, b.value(E - 1, LAG_M, e))
                if e <= 3:
                    if some(b.value(SUM_STEPS, LAG_F, 1)):
                        act.wait_ge(sum_steps, b.value(SUM_STEPS, LAG_F, e + 3))
                else:
                    act.wait_ge(sum_steps, b.value(SUM_STEPS, LAG_M, max(e - 5, 1)))
                if e == 1:
                    act.wait_ge(gate_steps, b.value(GATE_STEPS, LAG_M, GATE_STEPS))
                bank = (b.slot(LAG_M, 2) * (E - 1) + e - 1) % 2
                for j in range(TILES):
                    last = nc.scalar.activation(term[:, slot, j * D:(j + 1) * D], ps_e[:, bank, j, :],
                                                ACT.Identity, scale=gate[:, b.slot(LAG_M, 2), j, e:e + 1])
                last.then_inc(term_ready, 1)

            def beat(b):
                if b.turn is None:
                    for p in pieces_in(b.k):
                        _, hi, _, n = pieces_of(p)
                        act.wait_ge(raw_loaded[p % RAW_SLOTS], 16 * (p // RAW_SLOTS + 1))
                        copy(hi, term[:, p % RAW_SLOTS, 0:n]).then_inc(split_hi, 1)
                if b.turn is None and b.k == LAG_M:
                    act.wait_ge(split_lo, PIECES)
                if b.has(LAG_M):
                    act.wait_ge(gate_steps, b.value(GATE_STEPS, LAG_M, 7))
                    nc.scalar.activation(gexp[:], gdiff[:], ACT.Exp).then_inc(gexp_ready, 1)
                if 0 <= b.k <= LIF_BEATS:
                    act.wait_ge(lif, b.value(2 * STEPS, 0, 1 if b.lif() else 0))
                fill = 0
                if b.has(LAG_RKV):
                    for f in range(3):
                        to_lif(b, f, 2 * f * B, 2, None)
                    fill += 3
                if b.has(LAG_S):
                    to_lif(b, fill, COL_H2, 2, C_B2)
                    fill += 1
                if b.has(LAG_Y):
                    read_x1(b)
                if b.has(LAG_M):
                    read_expert(b, 1)
                    read_expert(b, 2)
                if b.has(LAG_Y):
                    for f in range(4):
                        to_lif(b, fill + f, COL_H1 + 2 * f * B, 2, C_B1 + 2 * f)
                if b.has(LAG_Z):
                    act.wait_ge(x3T_done, b.value(1, LAG_Z, 1))
                    if some(b.value(E - 1, LAG_Z + 2, E - 1)):
                        act.wait_ge(expert_done, b.value(E - 1, LAG_Z + 2, E - 1))
                    copy(x3_hi[:, b.slot(LAG_Z, 2)], ps_zx[:]).then_inc(x3_hi_ready, 1)
                if b.has(LAG_M):
                    read_expert(b, 3)
                    act.wait_ge(gateT_done, b.value(1, LAG_M, 1))
                    if some(b.value(1, LAG_M)):
                        act.wait_ge(bias_done, b.value(1, LAG_M))
                    copy(gate_T[:], ps_zx[0:E, :, 0:P]).then_inc(gateT_ready, 1)
                    for e in range(4, E):
                        read_expert(b, e)

            act.wait_ge(fixed_loaded, 32)
            act.wait_ge(vec_set, 4)
            run_beats(act, beat)

        @block.vector
        def _(dve):
            v = nc.vector

            def spikes_view(slot, tile, tiles):
                return U[:, slot, :, tile * B:(tile + tiles) * B]

            def lif_membrane(b, t, c0, c1):
                s = b.k % 2
                before = X[:, s, t - 1, c0:c1] if t else X[:, 1 - s, STEPS - 1, c0:c1]
                dve.wait_ge(lif, b.value(2 * STEPS, 0, 2 * t))
                v.scalar_tensor_tensor(out=U[:, s, t, c0:c1], in0=before, scalar=0.5, in1=X[:, s, t, c0:c1],
                                       op0=ALU.mult, op1=ALU.add).then_inc(lif, 1)

            def lif_reset(b, t, c0, c1):
                s = b.k % 2
                u = U[:, s, t, c0:c1]
                dve.wait_ge(lif, b.value(2 * STEPS, 0, 2 * t + 1))
                v.scalar_tensor_tensor(out=X[:, s, t, c0:c1], in0=u, scalar=THRESHOLD, in1=u,
                                       op0=ALU.is_lt, op1=ALU.mult).then_inc(lif, 1)

            def after(sem_, per, lag, b, n):
                dve.wait_ge(sem_, b.value(per, lag, n))

            def plain(b):
                if b.turn is not None:
                    dve.sem_inc(dve_waited, 1)

            def z_sum(b, k):
                if k == 0:
                    if some(b.value(1, LAG_Z)):
                        dve.wait_ge(zT_done, b.value(1, LAG_Z))
                    dve.wait_ge(x1_ready, b.value(3, LAG_Z, 3))
                s2 = U[:, (b.k - 1) % 2, :, COL_H2 + k * B:COL_H2 + (k + 1) * B]
                v.scalar_tensor_tensor(out=z[:, k, :].rearrange("p (t b) -> p t b", b=B), in0=s2,
                                       scalar=THRESHOLD,
                                       in1=x1[:, b.slot(LAG_Z, 4), k, :].rearrange("p (t b) -> p t b", b=B),
                                       op0=ALU.is_ge, op1=ALU.add).then_inc(z_ready, 1)

            def y_stage(b, step):
                slot = (b.k - 1) % 2
                chain = lambda n: after(y_steps, Y_STEPS, LAG_Y, b, n)
                if step == 0:
                    if some(b.value(1, LAG_Y)):
                        dve.wait_ge(attn_done, b.value(1, LAG_Y))
                    v.tensor_scalar(v_spikes, spikes_view(slot, 2 * DK, DK), THRESHOLD, None,
                                    ALU.is_ge).then_inc(y_steps, 1)
                if step == 1:
                    chain(1)
                    v.scalar_tensor_tensor(out=h[:], in0=spikes_view(slot, DK, DK).rearrange("p t c -> p c t"),
                                           scalar=THRESHOLD, in1=v_spikes.rearrange("p t c -> p c t"),
                                           op0=ALU.is_ge, op1=ALU.mult).then_inc(y_steps, 1)
                if step == 2:
                    chain(2)
                    v.scalar_tensor_tensor(out=h[:, :, 0], in0=h_last[:], scalar=DECAY, in1=h[:, :, 0],
                                           op0=ALU.mult, op1=ALU.add).then_inc(y_steps, 1)
                if step == 3:
                    chain(3)
                    hv = h[:].rearrange("p c t -> p (c t)")
                    v.tensor_tensor_scan(hv, decay[:].rearrange("p c t -> p (c t)"), hv, 0.0,
                                         ALU.mult, ALU.add).then_inc(y_steps, 1)
                if step == 4:
                    chain(4)
                    v.tensor_copy(h_last[:], h[:, :, STEPS - 1]).then_inc(y_steps, 1)
                    for k in range(DK):
                        v.scalar_tensor_tensor(out=y[:, k * N:(k + 1) * N].rearrange("p (t b) -> p t b", b=B),
                                               in0=spikes_view(slot, k, 1), scalar=THRESHOLD,
                                               in1=h[:, k * B:(k + 1) * B, :].rearrange("p c t -> p t c"),
                                               op0=ALU.is_ge, op1=ALU.mult).then_inc(y_steps, 1)

            def bn_stats(ln, j, src, steps):
                v.bn_stats(stats[ln][:, j, :], src).then_inc(steps, 1)

            def bn_aggr(b, ln, steps, per, lag, done):
                after(steps, per, lag, b, done)
                plain(b)
                for j in range(TILES):
                    v.bn_aggr(mv[ln][:, j, :], stats[ln][:, j, :]).then_inc(steps, 1)

            def normalise(b, ln, dst, src, steps, lag):
                dve.wait_ge(rstd_ready[ln], b.value(2, lag, 2))
                for j in range(TILES):
                    v.tensor_scalar(dst[:, j, :], src[:, j, :], mv[ln][:, j, 0:1], rstd[ln][:, j:j + 1],
                                    ALU.subtract, ALU.mult).then_inc(steps, 1)

            def ln1_sum(b):
                dve.wait_ge(attn_done, b.value(1, LAG_Y, 1))
                dve.wait_ge(xa_loaded, b.value(16, LAG_Y, 16))
                if some(b.value(1, LAG_Y)):
                    dve.wait_ge(x1T_done, b.value(1, LAG_Y))
                v.tensor_tensor(x1n[:], xa[:], ps_attn[:], ALU.add).then_inc(ln1_steps, 1)

            def ln2_scale(b, j):
                v.scalar_tensor_tensor(out=w[:, j, :], in0=ps_zx[:, j, :], scalar=mv[1][:, j, 0:1],
                                       in1=ln2_gain, op0=ALU.subtract, op1=ALU.mult).then_inc(ln2_steps, 1)

            def ln2_add(b, j):
                v.scalar_tensor_tensor(out=w[:, j, :], in0=w[:, j, :], scalar=rstd[1][:, j:j + 1],
                                       in1=xb[:, j, :], op0=ALU.mult, op1=ALU.add).then_inc(ln2_steps, 1)

            def x3_low(b):
                dve.wait_ge(x3_hi_ready, b.value(1, LAG_Z, 1))
                s = b.slot(LAG_Z, 2)
                if some(b.value(E - 1, LAG_Z + 2, E - 1)):
                    dve.wait_ge(expert_done, b.value(E - 1, LAG_Z + 2, E - 1))
                v.tensor_tensor(x3_lo[:, s], ps_zx[:], x3_hi[:, s].bitcast(F32),
                                ALU.subtract).then_inc(x3_lo_ready, 1)

            def gate_stage(b, step):
                gslot = b.slot(LAG_M, 2)
                chain = lambda n: after(gate_steps, GATE_STEPS, LAG_M, b, n)
                if step == 0:
                    dve.wait_ge(e0_done, b.value(1, LAG_M, 1))
                    v.tensor_tensor(logit[:], ps_e0[:, :, D:D + E],
                                    cst[:, C_BG:C_BG + TILES * E].rearrange("p (j e) -> p j e", e=E),
                                    ALU.add).then_inc(gate_steps, 1)
                if step == 1:
                    chain(1)
                    plain(b)
                    for j in range(TILES):
                        v.max(top[:, j, :], logit[:, j, :]).then_inc(gate_steps, 1)
                if step == 2:
                    chain(3)
                    plain(b)
                    for j in range(TILES):
                        v.max_index(top_at[:, j, :], top[:, j, :], logit[:, j, :]).then_inc(gate_steps, 1)
                if step == 3:
                    chain(5)
                    v.tensor_copy(top_atf[:], top_at[:, :, 0:2]).then_inc(gate_steps, 1)
                    if some(b.value(1, LAG_M)):
                        dve.wait_ge(gexp_ready, b.value(1, LAG_M))
                    v.tensor_tensor(gdiff[:], top[:, :, 1], top[:, :, 0], ALU.subtract).then_inc(gate_steps, 1)
                if step == 4:
                    dve.wait_ge(gexp_ready, b.value(1, LAG_M, 1))
                    v.tensor_scalar(gden[:], gexp[:], 1.0, None, ALU.add).then_inc(gate_steps, 1)
                if step == 5:
                    chain(8)
                    v.reciprocal(g1st[:], gden[:]).then_inc(gate_steps, 1)
                if step == 6:
                    chain(9)
                    v.tensor_tensor(g2nd[:], gexp[:], g1st[:], ALU.mult).then_inc(gate_steps, 1)
                if step in (7, 8):
                    chain(10)
                    if step == 7:
                        if some(b.value(E - 1, LAG_M + 2, E - 1)):
                            dve.wait_ge(term_ready, b.value(E - 1, LAG_M + 2, E - 1))
                        if some(b.value(1, LAG_M + 2, 1)):
                            dve.wait_ge(gateT_done, b.value(1, LAG_M + 2, 1))
                    dst, at, weight = ((gate[:, gslot], 0, g1st), (gate_b[:], 1, g2nd))[step - 7]
                    for j in range(TILES):
                        v.tensor_scalar(dst[:, j, :], cst[:, C_IOTA:C_IOTA + E], top_atf[:, j, at:at + 1],
                                        weight[:, j:j + 1], ALU.is_equal, ALU.mult).then_inc(gate_steps, 1)
                if step == 9:
                    chain(14)
                    v.tensor_tensor(gate[:, gslot], gate[:, gslot], gate_b[:], ALU.add).then_inc(gate_steps, 1)

            def add_e0(b, j):
                if j == 0:
                    dve.wait_ge(gate_steps, b.value(GATE_STEPS, LAG_M, GATE_STEPS))
                    if some(b.value(SUM_STEPS, LAG_M)):
                        dve.wait_ge(sum_steps, b.value(SUM_STEPS, LAG_M))
                v.scalar_tensor_tensor(out=acc[:, j, :], in0=ps_e0[:, j, 0:D],
                                       scalar=gate[:, b.slot(LAG_M, 2), j, 0:1], in1=x3[:, j, :],
                                       op0=ALU.mult, op1=ALU.add).then_inc(e0_added, 1)

            def fin_stage(b, step):
                chain = lambda n: after(fin_steps, FIN_STEPS, LAG_F, b, n)
                if step == 0:
                    dve.wait_ge(bias_done, b.value(1, LAG_F, 1))
                    dve.wait_ge(e0_added, b.value(2, LAG_F, 2))
                    v.tensor_tensor(acc[:], acc[:], ps_zx[:], ALU.add).then_inc(fin_steps, 1)
                if step == 1:
                    dve.wait_ge(sum_steps, b.value(SUM_STEPS, LAG_F, SUM_STEPS))
                    for j in range(TILES):
                        bn_stats(3, j, res[:, j, :], fin_steps)
                if step == 2:
                    bn_aggr(b, 3, fin_steps, FIN_STEPS, LAG_F, 3)
                if step == 3:
                    normalise(b, 3, res, res, fin_steps, LAG_F)

            def side(b, slot):
                has_y, has_z, has_m, has_f = (b.has(g) for g in (LAG_Y, LAG_Z, LAG_M, LAG_F))
                if slot == 0 and (has_y or has_z):
                    if some(b.value(2 * STEPS, 0)):
                        dve.wait_ge(lif, b.value(2 * STEPS, 0))
                if has_z and slot == 0:
                    z_sum(b, 0)
                    z_sum(b, 1)
                if has_y and 1 <= slot <= 5:
                    y_stage(b, slot - 1)
                if has_f and slot == 6:
                    fin_stage(b, 0)
                if has_m and 7 <= slot <= 10:
                    gate_stage(b, slot - 7)
                if has_y:
                    if slot == 11:
                        ln1_sum(b)
                    if slot == 12:
                        after(ln1_steps, LN1_STEPS, LAG_Y, b, 1)
                        bn_stats(0, 0, x1n[:, 0, :], ln1_steps)
                    if slot == 13:
                        bn_stats(0, 1, x1n[:, 1, :], ln1_steps)
                    if slot == 14:
                        bn_aggr(b, 0, ln1_steps, LN1_STEPS, LAG_Y, 3)
                    if slot == 18:
                        normalise(b, 0, x1n, x1n, ln1_steps, LAG_Y)
                if has_z:
                    if slot == 15:
                        dve.wait_ge(zT_done, b.value(1, LAG_Z, 1))
                        bn_stats(1, 0, ps_zx[:, 0, :], ln2_steps)
                    if slot == 16:
                        bn_stats(1, 1, ps_zx[:, 1, :], ln2_steps)
                    if slot == 17:
                        bn_aggr(b, 1, ln2_steps, LN2_STEPS, LAG_Z, 2)
                if has_m:
                    if slot in (15, 16, 17):
                        gate_stage(b, slot - 11)
                    if slot in (19, 20, 21):
                        gate_stage(b, slot - 12)
                if has_z:
                    if slot == 22:
                        after(ln2_steps, LN2_STEPS, LAG_Z, b, 4)
                        ln2_scale(b, 0)
                    if slot == 23:
                        ln2_scale(b, 1)
                    if slot == 24:
                        after(ln2_steps, LN2_STEPS, LAG_Z, b, 6)
                        dve.wait_ge(rstd_ready[1], b.value(2, LAG_Z, 2))
                        dve.wait_ge(xb_ready, b.value(1, LAG_Z, 1))
                        ln2_add(b, 0)
                        ln2_add(b, 1)
                    if slot == 25:
                        after(ln2_steps, LN2_STEPS, LAG_Z, b, 8)
                        bn_stats(2, 0, w[:, 0, :], ln3_steps)
                        bn_stats(2, 1, w[:, 1, :], ln3_steps)
                    if slot == 26:
                        bn_aggr(b, 2, ln3_steps, LN3_STEPS, LAG_Z, 2)
                if has_m and slot in (26, 27):
                    add_e0(b, slot - 26)
                if has_z and slot == 28:
                    if has_m:
                        dve.wait_ge(e0_added, b.value(2, LAG_M, 2))
                    if some(b.value(1, LAG_Z)):
                        dve.wait_ge(x3T_done, b.value(1, LAG_Z))
                    normalise(b, 2, x3, w, ln3_steps, LAG_Z)
                if has_f and slot == 29:
                    fin_stage(b, 1)
                if has_f and slot == 30:
                    fin_stage(b, 2)
                if has_z and slot == 31:
                    x3_low(b)
                if has_f and slot == 31:
                    fin_stage(b, 3)

            def lif_columns(b):
                if b.turn is not None:
                    return 0, COLS
                has = [0 <= b.k - lag < CHUNKS for lag in (0, 2, 4)]
                edges = [0, COL_H1, COL_H2, COLS]
                return edges[has.index(True)], edges[3 - has[::-1].index(True)]

            def beat(b):
                if b.lif():
                    c0, c1 = lif_columns(b)
                    if some(b.fills()):
                        dve.wait_ge(proj_read, b.fills())
                    if some(b.value(4, LAG_S, 0) if b.turn is not None else 4 * min(max(b.k - LAG_S, 0), CHUNKS)):
                        dve.wait_ge(s1_ready, b.value(4, LAG_S, 0) if b.turn is not None else 4 * min(max(b.k - LAG_S, 0), CHUNKS))
                    for t in range(STEPS):
                        lif_membrane(b, t, c0, c1)
                        side(b, 2 * t)
                        lif_reset(b, t, c0, c1)
                        side(b, 2 * t + 1)
                else:
                    for slot in range(2 * STEPS):
                        side(b, slot)

            v.memset(X[:, 1, STEPS - 1, :], 0.0).then_inc(vec_set, 1)
            v.memset(h_last[:], 0.0).then_inc(vec_set, 1)
            v.memset(decay[:], DECAY).then_inc(vec_set, 1)
            dve.wait_ge(vec_set, 3)
            v.memset(decay[:, :, 0], 0.0).then_inc(vec_set, 1)
            dve.wait_ge(vec_set, 4)
            dve.wait_ge(fixed_loaded, 32)
            run_beats(dve, beat)

        @block.gpsimd
        def _(pool):
            g = nc.gpsimd

            def plain(b):
                if b.turn is not None:
                    pool.sem_inc(pool_waited, 1)

            def reciprocal_std(b, ln, steps, per, lag, done):
                pool.wait_ge(steps, b.value(per, lag, done))
                plain(b)
                g.tensor_scalar(veps[ln][:], mv[ln][:, :, 1], EPS, None, ALU.add).then_inc(rstd_ready[ln], 1)
                pool.wait_ge(rstd_ready[ln], b.value(2, lag, 1))
                g.tensor_tensor(rstd[ln][:], veps[ln][:], neg_half[:], ALU.pow).then_inc(rstd_ready[ln], 1)

            def spikes_h1(b, part):
                if part == 0:
                    if some(b.value(2 * STEPS, 0)):
                        pool.wait_ge(lif, b.value(2 * STEPS, 0))
                    if some(b.fills()):
                        pool.wait_ge(proj_filled, b.fills())
                    plain(b)
                for e in range(2):
                    ft = 2 * part + e
                    last = g.tensor_scalar(s1[:, ft, :].rearrange("p (t b) -> p t b", b=B),
                                           U[:, (b.k - 1) % 2, :, COL_H1 + ft * B:COL_H1 + (ft + 1) * B],
                                           THRESHOLD, None, ALU.is_ge)
                last.then_inc(s1_ready, 1)

            def add_term(b, lag, e):
                pool.wait_ge(term_ready, b.value(E - 1, lag, e))
                if e == 2:
                    if some(b.value(SUM_STEPS, lag)):
                        pool.wait_ge(sum_steps, b.value(SUM_STEPS, lag))
                    first = term[:, 0, 0:PIECE]
                else:
                    pool.wait_ge(sum_steps, b.value(SUM_STEPS, lag, e - 2))
                    first = psum_terms[:].rearrange("p j d -> p (j d)")
                g.tensor_tensor(psum_terms[:].rearrange("p j d -> p (j d)"), first,
                                term[:, (e - 1) % RAW_SLOTS, 0:PIECE], ALU.add).then_inc(sum_steps, 1)

            def add_all(b):
                pool.wait_ge(sum_steps, b.value(SUM_STEPS, LAG_F, SUM_STEPS - 1))
                pool.wait_ge(fin_steps, b.value(FIN_STEPS, LAG_F, 1))
                if some(b.value(16, LAG_F)):
                    pool.wait_ge(out_stored, b.value(16, LAG_F))
                g.tensor_tensor(res[:], acc[:], psum_terms[:], ALU.add).then_inc(sum_steps, 1)

            def beat(b):
                if b.turn is None:
                    for p in pieces_in(b.k):
                        _, hi, lo, n = pieces_of(p)
                        pool.wait_ge(split_hi, p + 1)
                        g.tensor_tensor(lo, term[:, p % RAW_SLOTS, 0:n], hi.bitcast(F32),
                                        ALU.subtract).then_inc(split_lo, 1)
                if b.has(LAG_Z):
                    pool.wait_ge(xb_loaded, b.value(16, LAG_Z, 16))
                    for j in range(TILES):
                        last = g.tensor_tensor(xb[:, j, :], xb[:, j, :], ln2_bias, ALU.add)
                    last.then_inc(xb_ready, 1)
                for part in range(4):
                    if b.has(LAG_S):
                        spikes_h1(b, part)
                    if b.has(LAG_F):
                        add_term(b, LAG_F, 4 + part)
                if b.has(LAG_F):
                    add_all(b)
                if b.has(LAG_Y):
                    reciprocal_std(b, 0, ln1_steps, LN1_STEPS, LAG_Y, 5)
                if b.has(LAG_Z):
                    reciprocal_std(b, 1, ln2_steps, LN2_STEPS, LAG_Z, 4)
                if b.has(LAG_Y):
                    pool.wait_ge(x1_ready, b.value(3, LAG_Y, 3))
                    g.tensor_tensor(x1_lo[:], x1[:, b.slot(LAG_Y, 4)], x1_hi[:].bitcast(F32),
                                    ALU.subtract).then_inc(x1_lo_ready, 1)
                if b.has(LAG_M):
                    add_term(b, LAG_M, 2)
                if b.has(LAG_Z):
                    reciprocal_std(b, 2, ln3_steps, LN3_STEPS, LAG_Z, 4)
                if b.has(LAG_F):
                    reciprocal_std(b, 3, fin_steps, FIN_STEPS, LAG_F, 5)
                if b.has(LAG_M):
                    add_term(b, LAG_M, 3)

            g.memset(neg_half[:], -0.5).then_inc(pool_set, 1)
            pool.wait_ge(pool_set, 1)
            pool.wait_ge(fixed_loaded, 32)
            run_beats(pool, beat)


def kernel(**inputs):
    import numpy as np
    import concourse.bacc as bacc
    from concourse.bass_utils import run_bass_kernel_spmd

    a = {k: np.asarray(v) for k, v in inputs.items()}
    x = a["L0_attn_x"]
    by_time = x.transpose(1, 0, 2).reshape(CHUNKS, N, D)
    col = lambda v, n: v.reshape(n, P).T
    wide = lambda v: np.broadcast_to(v.reshape(1, -1), (P, v.size))
    k_first = lambda m: m.reshape(m.shape[0] // P, P, m.shape[1]).transpose(1, 0, 2)
    w_qkv = np.concatenate([a["L0_attn_Wr"], a["L0_attn_Wk"], a["L0_attn_Wv"]], axis=0)
    we = a["L0_ffn_We"]
    bias_rows = np.concatenate([a["L0_ffn_be"], np.zeros((P - E, D), np.float32)], axis=0)
    consts = np.concatenate([
        col(a["L0_attn_b1"], FK), col(a["L0_attn_b2"], DK), col(a["L0_attn_ln1_g"], DK),
        col(a["L0_attn_ln1_b"], DK), wide(a["L0_ffn_bg"]), wide(a["L0_ffn_bg"]),
        wide(np.arange(E, dtype=np.float32)), np.eye(P, dtype=np.float32),
        wide(a["L0_attn_ln2_g"]), wide(a["L0_attn_ln2_b"]), bias_rows], axis=1)
    arrays = {
        "x_T": by_time.transpose(0, 2, 1).reshape(CHUNKS, DK, P, N).transpose(0, 2, 1, 3),
        "x_tok": by_time.reshape(CHUNKS, TILES, P, D).transpose(0, 2, 1, 3),
        "w_rkv": k_first(w_qkv.T),
        "w_o": k_first(a["L0_attn_Wo"].T),
        "w_1": k_first(a["L0_attn_W1"].T).reshape(P, DK * F),
        "w_2": k_first(a["L0_attn_W2"].T).reshape(P, FK * D),
        "w_e0": k_first(np.concatenate([we[0], a["L0_ffn_Wg"]], axis=1)).reshape(P, PIECE0),
        "w_e": np.stack([k_first(we[e]).reshape(P, PIECE) for e in range(1, E)]),
        "consts": consts,
    }
    nc = bacc.Bacc("TRN2", target_bir_lowering=False, num_devices=1)
    args = []
    for name in arrays:
        arrays[name] = np.ascontiguousarray(arrays[name])
        args.append(nc.dram_tensor(name, arrays[name].shape, F32, kind="ExternalInput").ap())
    out = nc.dram_tensor("out", (CHUNKS, P, TILES, D), F32, kind="ExternalOutput").ap()
    build(nc, *args, out)
    r = run_bass_kernel_spmd(nc, [arrays], core_ids=[0])
    got = np.asarray(r.results[0]["out"])
    return got.transpose(0, 2, 1, 3).reshape(T, B, D).transpose(1, 0, 2)
```

```python
from contextlib import ExitStack

import concourse.bass as bass
from concourse import mybir

F32 = mybir.dt.float32
F32R = mybir.dt.float32r
U32 = mybir.dt.uint32
ALU = mybir.AluOpType
ACT = mybir.ActivationFunctionType

P = 128
B, T, D, F, E = 16, 512, 256, 1024, 8
STEPS = 16
N = STEPS * B
CHUNKS = T // STEPS
TILES = N // P
DK = D // P
FK = F // P
RKV_TILES = 3 * DK
EPS = 1e-5
THRESHOLD = 2.0
DECAY = 0.9

COL_H1 = RKV_TILES * B
COL_H2 = COL_H1 + FK * B
COLS = COL_H2 + DK * B

LAG_X = -2
LAG_RKV = -1
LAG_Y = 1
LAG_S = 3
LAG_Z = 5
LAG_M = 6
LAG_F = 7
LIF_BEATS = CHUNKS + 4
FIRST_STEADY = LAG_F
UNROLL = 4
STEADY_TURNS = (CHUNKS - 1 + LAG_RKV + 1 - FIRST_STEADY) // UNROLL
FIRST_DRAIN = FIRST_STEADY + UNROLL * STEADY_TURNS
LAST_FULL = CHUNKS - 1 + LAG_Y
LAST_BEAT = CHUNKS - 1 + LAG_F

C_B1, C_B2, C_G1, C_BE1 = 0, FK, FK + DK, FK + 2 * DK
C_BG = C_BE1 + DK
C_IOTA = C_BG + TILES * E
C_ID = C_IOTA + E
C_G2 = C_ID + P
C_BE2 = C_G2 + D
C_BEXP = C_BE2 + D
C_ALL = C_BEXP + D

PIECE = DK * D
PIECE0 = DK * (D + E)
W1_PIECES = DK * F // PIECE
W2_PIECES = FK * D // PIECE
PIECES = W1_PIECES + W2_PIECES + E
RAW_SLOTS = 4
ROW_HH, ROW_LH, ROW_HL = 0, 32, 64
STACK = ROW_HL + E


STEADY = dict(y=(0, 1, 2, 3, 4), z_sum=5, spikes_h1=7, fin_sum=5,
              gate=(6, 7, 8, 9, 12, 13, 14, 14, 15, 16, 18, 20), add_e0=(18, 22),
              ln1_sum=7, ln1_stats=(8, 9), ln1_aggr=10, ln1_norm=13,
              ln2_stats=(11, 12), ln2_aggr=13, ln2_scale=(16, 17), ln2_add=19,
              ln3_stats=20, ln3_aggr=21, ln3_shift=24, x3_low=30,
              fin_stats=25, fin_aggr=26, fin_shift=28)
FILL = dict(z_sum=-1, y=(-1,) * 5, spikes_h1=-1, fin_sum=-1,
            gate=(4, 5, 6, 7, 9, 10, 10, 11, 12, 13, 17, 18), add_e0=(14, 15),
            ln1_sum=2, ln1_stats=(3, 4), ln1_aggr=5, ln1_norm=9,
            ln2_stats=(0, 1), ln2_aggr=2, ln2_scale=(6, 7), ln2_add=8,
            ln3_stats=9, ln3_aggr=10, ln3_shift=16, x3_low=31,
            fin_stats=25, fin_aggr=26, fin_shift=31)
DRAIN = dict(z_sum=-1, y=(-1,) * 5, spikes_h1=-1, fin_sum=-1,
             gate=(-1, 0, 1, 2, 3, 4, 5, 6, 6, 7, 12, 13), add_e0=(11, 12),
             ln1_sum=-1, ln1_stats=(-1, -1), ln1_aggr=-1, ln1_norm=4,
             ln2_stats=(0, 1), ln2_aggr=2, ln2_scale=(2, 5), ln2_add=8,
             ln3_stats=9, ln3_aggr=10, ln3_shift=14, x3_low=26,
             fin_stats=16, fin_aggr=17, fin_shift=22)


class Beat:

    def __init__(self, k, turn=None):
        self.k, self.turn = k, turn

    @property
    def edge(self):
        return self.turn is None and (self.k < FIRST_STEADY or self.k > LAST_FULL)

    @property
    def halves(self):
        return self.turn is None and self.k < LAG_Z

    @property
    def dve_spikes(self):
        return FK if self.edge else 0

    def value(self, per, lag, add=0):
        n = per * (self.k - lag) + add
        return n if self.turn is None else self.turn * (UNROLL * per) + n

    def has(self, lag):
        return self.turn is not None or 0 <= self.k - lag < CHUNKS + (lag == LAG_X)

    def lif(self):
        return self.turn is not None or 0 <= self.k < LIF_BEATS

    def chunk(self, lag):
        return self.value(1, lag)

    def slot(self, lag, slots):
        return (self.k - lag) % slots

    def fills(self, add=0):
        if self.turn is not None:
            return self.turn * (UNROLL * 8) + 8 * self.k - 4 + add
        done = lambda lag: min(max(self.k - lag, 0), CHUNKS)
        return 3 * done(LAG_RKV) + 4 * done(LAG_Y) + done(LAG_S) + add

    def w2_fills(self):
        return self.fills(-4 if self.turn is not None or Beat(self.k - 1).has(LAG_Y) else 0)

    def loads(self, lag, slots):
        n = 16 * ((self.k - lag) // slots + 1)
        return n if self.turn is None else self.turn * (16 * UNROLL // slots) + n


def some(n):
    return not isinstance(n, int) or n > 0


def build(nc, x_T, x_tok, w_rkv, w_o, w_1, w_2, w_e0, w_e, consts, out):
    with ExitStack() as ctx:
        def sb(name, shape, dt=F32):
            return ctx.enter_context(nc.sbuf_tensor(name, shape, dt))

        def sem(name):
            return ctx.enter_context(nc.semaphore(name))

        wrkv_raw = sb("wrkv_raw", [P, 3, DK * D])
        wrkv_hi, wrkv_lo = sb("wrkv_hi", [P, 3, DK * D], F32R), sb("wrkv_lo", [P, 3, DK * D], F32R)
        wo = sb("wo", [P, DK, D])
        w1_hi, w1_lo = sb("w1_hi", [P, DK * F], F32R), sb("w1_lo", [P, DK * F], F32R)
        w2_hi, w2_lo = sb("w2_hi", [P, FK * D], F32R), sb("w2_lo", [P, FK * D], F32R)
        we0_hi, we0_lo = sb("we0_hi", [P, PIECE0], F32R), sb("we0_lo", [P, PIECE0], F32R)
        we_hi, we_lo = sb("we_hi", [P, E - 1, PIECE], F32R), sb("we_lo", [P, E - 1, PIECE], F32R)
        cst = sb("cst", [P, C_ALL])
        ident = cst[:, C_ID:C_ID + P]
        ln2_gain = cst[:, C_G2:C_G2 + D]
        ln2_bias = cst[:, C_BE2:C_BE2 + D]
        bias_raw = cst[0:STACK, C_BEXP:C_BEXP + D]
        bias_stack = sb("bias_stack", [STACK, D], F32R)
        decay = sb("decay", [P, DK * B, STEPS])
        neg_half = sb("neg_half", [P, TILES])
        U = sb("U", [P, 2, STEPS, COLS])
        V = sb("V", [P, COLS])
        xt = sb("xt", [P, 2, DK, N])
        x_hi, x_lo = sb("x_hi", [P, DK, N], F32R), sb("x_lo", [P, DK, N], F32R)
        xa = sb("xa", [P, TILES, D])
        h = sb("h", [P, DK * B, STEPS])
        h_last = sb("h_last", [P, DK * B])
        y = sb("y", [P, DK * N])
        v_spikes = y[:].rearrange("p (t c) -> p t c", t=STEPS)
        x1n = sb("x1n", [P, TILES, D])
        x1 = sb("x1", [P, 4, DK, N])
        x1_hi, x1_lo = sb("x1_hi", [P, DK, N], F32R), sb("x1_lo", [P, DK, N], F32R)
        s1 = sb("s1", [P, FK, N], F32R)
        z = sb("z", [P, DK, N])
        xb = sb("xb", [P, TILES, D])
        w = sb("w", [P, TILES, D])
        x3 = sb("x3", [P, TILES, D])
        x3_hi, x3_lo = sb("x3_hi", [P, 2, DK, N], F32R), sb("x3_lo", [P, 2, DK, N], F32R)
        term = sb("term", [P, RAW_SLOTS, PIECE0])
        psum_terms = sb("psum_terms", [P, TILES, D])
        acc = sb("acc", [P, 2, TILES, D])
        res = sb("res", [P, TILES, D])
        logit = sb("logit", [P, TILES, E])
        top = sb("top", [P, TILES, 8])
        top_at = sb("top_at", [P, TILES, 8], U32)
        top_atf = sb("top_atf", [P, TILES, 2])
        gdiff, gexp = sb("gdiff", [P, TILES]), sb("gexp", [P, TILES])
        gden, g1st, g2nd = sb("gden", [P, TILES]), sb("g1st", [P, TILES]), sb("g2nd", [P, TILES])
        gate_b = sb("gate_b", [P, TILES, E])
        gate = sb("gate", [P, 2, TILES, E])
        gate_parts = sb("gate_parts", [P, TILES, STACK], F32R)
        gate_T = sb("gate_T", [STACK, TILES, P], F32R)
        stats = [sb(f"stats{i}", [P, TILES, 6]) for i in range(4)]
        mv = [sb(f"mv{i}", [P, TILES, 2]) for i in range(4)]
        veps = [sb(f"veps{i}", [P, TILES]) for i in range(4)]
        shift = [sb(f"shift{i}", [P, TILES]) for i in range(4)]
        rstd = [sb(f"rstd{i}", [P, TILES]) for i in range(4)]

        ps_proj = ctx.enter_context(nc.psum_tensor("ps_proj", [P, 2, 2, N], F32))
        ps_attn = ctx.enter_context(nc.psum_tensor("ps_attn", [P, 2, 256], F32))
        ps_zx = ctx.enter_context(nc.psum_tensor("ps_zx", [P, 2, 256], F32))
        ps_e0 = ctx.enter_context(nc.psum_tensor("ps_e0", [P, TILES, 512], F32))
        ps_e = ctx.enter_context(nc.psum_tensor("ps_e", [P, 2, TILES, D], F32))

        consts_loaded = sem("consts_loaded")
        wrkv_loaded = [sem(f"wrkv_loaded{f}") for f in range(3)]
        wrkv_hi_ready, wrkv_lo_ready = sem("wrkv_hi_ready"), sem("wrkv_lo_ready")
        x_hi_ready, x_lo_ready = sem("x_hi_ready"), sem("x_lo_ready")
        bias_hi_ready, bias_lo_ready = sem("bias_hi_ready"), sem("bias_lo_ready")
        wo_loaded = sem("wo_loaded")
        raw_loaded = [sem(f"raw_loaded{i}") for i in range(RAW_SLOTS)]
        split_hi, split_lo = sem("split_hi"), sem("split_lo")
        xt_loaded = [sem("xt_loaded0"), sem("xt_loaded1")]
        xa_loaded, xb_loaded = sem("xa_loaded"), sem("xb_loaded")
        out_stored = sem("out_stored")
        vec_set, pool_set = sem("vec_set"), sem("pool_set")
        proj_filled, proj_read = sem("proj_filled"), sem("proj_read")
        lif, lif_half = sem("lif"), sem("lif_half")
        y_steps, attn_done, ln1_steps = sem("y_steps"), sem("attn_done"), sem("ln1_steps")
        x1T_done, x1_ready = sem("x1T_done"), sem("x1_ready")
        x1_hi_ready, x1_lo_ready = sem("x1_hi_ready"), sem("x1_lo_ready")
        s1_ready = sem("s1_ready")
        z_ready, zT_done, xb_ready = sem("z_ready"), sem("zT_done"), sem("xb_ready")
        ln2_steps, ln3_steps = sem("ln2_steps"), sem("ln3_steps")
        x3T_done, x3_hi_ready, x3_lo_ready = sem("x3T_done"), sem("x3_hi_ready"), sem("x3_lo_ready")
        rstd_ready = [sem(f"rstd_ready{i}") for i in range(4)]
        e0_done, expert_done = sem("e0_done"), sem("expert_done")
        gate_steps, gexp_ready = sem("gate_steps"), sem("gexp_ready")
        gateT_done, gateT_ready, bias_done = sem("gateT_done"), sem("gateT_ready"), sem("bias_done")
        e0_added, term_ready, sum_steps = sem("e0_added"), sem("term_ready"), sem("sum_steps")
        fin_steps, x3_ready, res_ready = sem("fin_steps"), sem("x3_ready"), sem("res_ready")
        dve_waited, pool_waited = sem("dve_waited"), sem("pool_waited")

        Y_STEPS, LN1_STEPS, LN2_STEPS, LN3_STEPS, GATE_STEPS, FIN_STEPS, SUM_STEPS = 7, 7, 8, 5, 17, 6, 7
        GATES_DONE = 15

        def pieces_of(p):
            if p < W1_PIECES:
                s = slice(p * PIECE, (p + 1) * PIECE)
                return w_1[:, s], w1_hi[:, s], w1_lo[:, s], PIECE
            p -= W1_PIECES
            if p < W2_PIECES:
                s = slice(p * PIECE, (p + 1) * PIECE)
                return w_2[:, s], w2_hi[:, s], w2_lo[:, s], PIECE
            p -= W2_PIECES
            if p == 0:
                return w_e0, we0_hi[:, :], we0_lo[:, :], PIECE0
            return w_e[p - 1], we_hi[:, p - 1, :], we_lo[:, p - 1, :], PIECE

        def pieces_in(k):
            per = {-1: range(0, 4), 0: range(4, 8), 1: range(8, 11), 2: range(11, 14), 3: range(14, 16)}
            return per.get(k, range(0))

        def run_beats(eng, beat):
            for k in range(LAG_X, FIRST_STEADY):
                beat(Beat(k))
            with eng.Fori(0, STEADY_TURNS) as turn:
                for u in range(UNROLL):
                    beat(Beat(FIRST_STEADY + u, turn))
            for k in range(FIRST_DRAIN, LAST_BEAT + 1):
                beat(Beat(k))

        block = ctx.enter_context(nc.Block())

        @block.sync
        def _(sp):
            def load_xt(b):
                if some(b.value(1, LAG_X + 1)):
                    sp.wait_ge(x_lo_ready, b.value(1, LAG_X + 1))
                s = b.slot(LAG_X, 2)
                sp.dma_start(xt[:, s], x_T[b.chunk(LAG_X)]).then_inc(xt_loaded[s], 16)


            def beat(b):
                if b.has(LAG_X):
                    load_xt(b)
                if b.turn is None and b.k == LAG_X:
                    for f in range(3):
                        sp.dma_start(wrkv_raw[:, f, :], w_rkv[f]).then_inc(wrkv_loaded[f], 16)
                    sp.dma_start(cst[:], consts).then_inc(consts_loaded, 16)
                    sp.dma_start(wo[:], w_o).then_inc(wo_loaded, 16)
                if b.turn is None:
                    for p in pieces_in(b.k):
                        src, _, _, n = pieces_of(p)
                        if some(p - RAW_SLOTS + 1):
                            sp.wait_ge(split_lo, p - RAW_SLOTS + 1)
                        sp.dma_start(term[:, p % RAW_SLOTS, 0:n], src).then_inc(raw_loaded[p % RAW_SLOTS], 16)
                if b.has(LAG_Y - 1):
                    if some(b.value(LN1_STEPS, LAG_Y, 1)):
                        sp.wait_ge(ln1_steps, b.value(LN1_STEPS, LAG_Y, 1))
                    sp.dma_start(xa[:], x_tok[b.chunk(LAG_Y - 1)]).then_inc(xa_loaded, 16)
                if b.has(LAG_Z - 1):
                    if some(b.value(LN2_STEPS, LAG_Z, LN2_STEPS)):
                        sp.wait_ge(ln2_steps, b.value(LN2_STEPS, LAG_Z, LN2_STEPS))
                    sp.dma_start(xb[:], x_tok[b.chunk(LAG_Z - 1)]).then_inc(xb_loaded, 16)

            run_beats(sp, beat)

        @block.tensor
        def _(pe):
            def split_product(dst, parts):
                mm, n = None, 3 * len(parts)
                i = 0
                for a_hi, a_lo, b_hi, b_lo in parts:
                    for lhs, rhs in ((a_hi, b_hi), (a_lo, b_hi), (a_hi, b_lo)):
                        mm = pe.matmul(dst, lhs, rhs, start=(i == 0), stop=(i == n - 1))
                        i += 1
                return mm

            def proj_bank(b, fill):
                if some(b.fills(fill - 1)):
                    pe.wait_ge(proj_read, b.fills(fill - 1))
                base = b.fills() if b.turn is None else 0
                return (base + fill) % 2

            def rkv(b, f):
                if f == 0:
                    pe.wait_ge(x_lo_ready, b.value(1, LAG_RKV, 1))
                if b.turn is None and b.k == LAG_RKV:
                    pe.wait_ge(wrkv_lo_ready, f + 1)
                bank = proj_bank(b, f)
                for e in range(2):
                    def cols(k):
                        c = k * D + e * P
                        return slice(c, c + P)
                    mm = split_product(ps_proj[:, bank, e, :],
                                       [(wrkv_hi[:, f, cols(k)], wrkv_lo[:, f, cols(k)], x_hi[:, k, :], x_lo[:, k, :])
                                        for k in range(DK)])
                mm.then_inc(proj_filled, 1)

            def attn(b):
                pe.wait_ge(y_steps, b.value(Y_STEPS, LAG_Y, Y_STEPS))
                if some(b.value(DK, LAG_Y)):
                    pe.wait_ge(x1_ready, b.value(DK, LAG_Y))
                if some(b.value(1, LAG_M)):
                    pe.wait_ge(gateT_ready, b.value(1, LAG_M))
                for j in range(TILES):
                    for k in range(DK):
                        mm = pe.matmul(ps_attn[:, j, :], y[:, k * N + j * P:k * N + (j + 1) * P],
                                       wo[:, k, :], start=(k == 0), stop=(k == DK - 1))
                mm.then_inc(attn_done, 1)

            def transpose4(dst, src_tile, done):
                for i in range(2):
                    for j in range(2):
                        mm = pe.transpose(dst[:, i, j * P:(j + 1) * P], src_tile(i, j), ident)
                mm.then_inc(done, 1)

            def w2(b, fill):
                bank = proj_bank(b, fill)
                pe.wait_ge(s1_ready, b.value(FK, LAG_S, FK))
                for e in range(DK):
                    for ft in range(FK):
                        for part, wp in enumerate((w2_hi, w2_lo)):
                            c = ft * D + e * P
                            mm = pe.matmul(ps_proj[:, bank, e, :], wp[:, c:c + P], s1[:, ft, :],
                                           start=(ft == 0 and part == 0), stop=(ft == FK - 1 and part == 1))
                mm.then_inc(proj_filled, 1)

            def w1(b, fill0):
                for f in range(4):
                    bank = proj_bank(b, fill0 + f)
                    def cols(k, e):
                        c = k * F + (2 * f + e) * P
                        return slice(c, c + P)
                    for e in range(2):
                        for k in range(DK):
                            if f == 0 and e == 0:
                                pe.wait_ge(x1_hi_ready, b.value(DK, LAG_Y, k + 1))
                            for wp in (w1_hi, w1_lo):
                                pe.matmul(ps_proj[:, bank, e, :], wp[:, cols(k, e)], x1_hi[:, k, :],
                                          start=(k == 0 and wp is w1_hi), stop=False)
                        for k in range(DK):
                            if f == 0 and e == 0:
                                pe.wait_ge(x1_lo_ready, b.value(DK, LAG_Y, k + 1))
                            mm = pe.matmul(ps_proj[:, bank, e, :], w1_hi[:, cols(k, e)], x1_lo[:, k, :],
                                           start=False, stop=(k == DK - 1))
                    mm.then_inc(proj_filled, 1)

            def x3_tile(b, lag, k, j):
                s = b.slot(lag, 2)
                return x3_hi[:, s, k, j * P:(j + 1) * P], x3_lo[:, s, k, j * P:(j + 1) * P]

            def expert0(b):
                pe.wait_ge(x3_lo_ready, b.value(1, LAG_M, 1))
                if some(b.value(2, LAG_M)):
                    pe.wait_ge(e0_added, b.value(2, LAG_M))
                for j in range(TILES):
                    mm = split_product(ps_e0[:, j, 0:D + E],
                                       [(*x3_tile(b, LAG_M, k, j), we0_hi[:, k * (D + E):(k + 1) * (D + E)],
                                         we0_lo[:, k * (D + E):(k + 1) * (D + E)]) for k in range(DK)])
                mm.then_inc(e0_done, 1)

            def expert(b, e):
                if some(b.value(E - 1, LAG_M, e - 2)):
                    pe.wait_ge(term_ready, b.value(E - 1, LAG_M, e - 2))
                bank = (b.slot(LAG_M, 2) * (E - 1) + e - 1) % 2
                for j in range(TILES):
                    mm = split_product(ps_e[:, bank, j, :],
                                       [(*x3_tile(b, LAG_M, k, j), we_hi[:, e - 1, k * D:(k + 1) * D],
                                         we_lo[:, e - 1, k * D:(k + 1) * D]) for k in range(DK)])
                mm.then_inc(expert_done, 1)

            def gates_T(b):
                pe.wait_ge(gate_steps, b.value(GATE_STEPS, LAG_M, GATE_STEPS))
                for j in range(TILES):
                    mm = pe.transpose(ps_attn[0:STACK, j, 0:P], gate_parts[:, j, :].bitcast(F32), ident)
                mm.then_inc(gateT_done, 1)

            def biases(b):
                pe.wait_ge(gateT_ready, b.value(1, LAG_M, 1))
                if b.has(LAG_Z):
                    pe.wait_ge(x3_lo_ready, b.value(1, LAG_Z, 1))
                if b.turn is None and b.k == LAG_M:
                    pe.wait_ge(bias_lo_ready, 1)
                for j in range(TILES):
                    mm = pe.matmul(ps_zx[:, j, :], gate_T[:, j, :], bias_stack[:], start=True, stop=True)
                mm.then_inc(bias_done, 1)

            def z_T(b):
                pe.wait_ge(z_ready, b.value(2, LAG_Z, 2))
                if b.has(LAG_F):
                    pe.wait_ge(fin_steps, b.value(FIN_STEPS, LAG_F, 1))
                transpose4(ps_zx, lambda j, k: z[:, k, j * P:(j + 1) * P], zT_done)

            def beat(b):
                edge = b.edge
                if b.has(LAG_Z) and edge and b.k < FIRST_STEADY:
                    z_T(b)
                if b.has(LAG_M) and b.k > LAG_M:
                    expert0(b)
                if b.has(LAG_Z) and edge and b.k > FIRST_STEADY:
                    z_T(b)
                if b.has(LAG_RKV) and not edge:
                    rkv(b, 0)
                if b.has(LAG_Y):
                    if b.turn is None and b.k == LAG_Y:
                        pe.wait_ge(wo_loaded, 16)
                        pe.wait_ge(consts_loaded, 16)
                    attn(b)
                if b.has(LAG_Z) and not edge:
                    z_T(b)
                if b.has(LAG_M) and b.k == LAG_M:
                    pe.wait_ge(split_lo, PIECES)
                    expert0(b)
                fill = 0
                if b.has(LAG_RKV):
                    for f in range(3):
                        if f or edge:
                            rkv(b, f)
                    fill += 3
                if b.has(LAG_S):
                    if b.turn is None and b.k == LAG_S:
                        pe.wait_ge(split_lo, W1_PIECES + W2_PIECES)
                    w2(b, fill)
                    fill += 1
                if b.has(LAG_Y):
                    pe.wait_ge(ln1_steps, b.value(LN1_STEPS, LAG_Y, LN1_STEPS))
                    transpose4(ps_attn, lambda k, j: x1n[:, j, k * P:(k + 1) * P], x1T_done)
                if b.has(LAG_M):
                    for e in (1, 2, 3):
                        expert(b, e)
                if b.has(LAG_Y):
                    if b.turn is None and b.k == LAG_Y:
                        pe.wait_ge(split_lo, W1_PIECES)
                    w1(b, fill)
                if b.has(LAG_M):
                    expert(b, 4)
                if b.has(LAG_Z):
                    pe.wait_ge(x3_ready, b.value(1, LAG_Z, 1))
                    transpose4(ps_zx, lambda k, j: x3[:, j, k * P:(k + 1) * P], x3T_done)
                if b.has(LAG_M):
                    gates_T(b)
                    for e in (5, 6, 7):
                        expert(b, e)
                    biases(b)

            run_beats(pe, beat)

        @block.scalar
        def _(act):
            def copy(out_, in_):
                return nc.scalar.activation(out_, in_, ACT.Identity)

            def to_lif(b, fill, col, tiles, bias):
                base = b.fills() if b.turn is None else 0
                bank = (base + fill) % 2
                dst = U[:, (b.k + 1) % 2, :, :]
                act.wait_ge(proj_filled, b.fills(fill + 1))
                if bias is None:
                    v = dst[:, :, col:col + tiles * B].rearrange("p t (g b) -> p g t b", b=B)
                    copy(v, ps_proj[:, bank, 0:tiles, :].rearrange("p g (t b) -> p g t b", b=B)).then_inc(proj_read, 1)
                    return
                for e in range(tiles):
                    last = nc.scalar.activation(dst[:, :, col + e * B:col + (e + 1) * B],
                                                ps_proj[:, bank, e, :].rearrange("p (t b) -> p t b", b=B),
                                                ACT.Identity, bias=cst[:, bias + e:bias + e + 1])
                last.then_inc(proj_read, 1)

            def read_x1(b):
                slot = b.slot(LAG_Y, 4)
                act.wait_ge(x1T_done, b.value(1, LAG_Y, 1))
                if some(b.value(2, LAG_Y + 4, 2)):
                    act.wait_ge(z_ready, b.value(2, LAG_Y + 4, 2))
                if some(b.fills()):
                    act.wait_ge(proj_filled, b.fills())
                for k in range(DK):
                    if k == 1 and b.has(LAG_M):
                        read_expert(b, 1)
                    for dst, done in ((x1_hi[:], x1_hi_ready), (x1[:, slot], x1_ready)):
                        nc.scalar.activation(dst[:, k, :], ps_attn[:, k, :], ACT.Identity,
                                             bias=cst[:, C_BE1 + k:C_BE1 + k + 1],
                                             scale=cst[:, C_G1 + k:C_G1 + k + 1]).then_inc(done, 1)

            def read_expert(b, e):
                slot = (e - 1) % RAW_SLOTS
                act.wait_ge(expert_done, b.value(E - 1, LAG_M, e))
                if e < RAW_SLOTS:
                    if some(b.value(SUM_STEPS, LAG_F, 1)):
                        act.wait_ge(sum_steps, b.value(SUM_STEPS, LAG_F, e + RAW_SLOTS - 1))
                elif e > RAW_SLOTS:
                    act.wait_ge(sum_steps, b.value(SUM_STEPS, LAG_M, max(e - RAW_SLOTS - 1, 1)))
                if e == 1:
                    act.wait_ge(gate_steps, b.value(GATE_STEPS, LAG_M, GATES_DONE))
                bank = (b.slot(LAG_M, 2) * (E - 1) + e - 1) % 2
                for j in range(TILES):
                    last = nc.scalar.activation(term[:, slot, j * D:(j + 1) * D], ps_e[:, bank, j, :],
                                                ACT.Identity, scale=gate[:, b.slot(LAG_M, 2), j, e:e + 1])
                last.then_inc(term_ready, 1)

            def split_x(b):
                act.wait_ge(xt_loaded[b.slot(LAG_X, 2)], b.loads(LAG_X, 2))
                if b.has(LAG_RKV):
                    act.wait_ge(proj_filled, b.fills(3))
                copy(x_hi[:], xt[:, b.slot(LAG_X, 2)]).then_inc(x_hi_ready, 1)

            def normalised(ln, dst, src):
                for j in range(TILES):
                    last = nc.scalar.activation(dst[:, j, :], src[:, j, :], ACT.Identity,
                                                bias=shift[ln][:, j:j + 1], scale=rstd[ln][:, j:j + 1])
                return last

            def norm_x3(b):
                act.wait_ge(ln3_steps, b.value(LN3_STEPS, LAG_Z, LN3_STEPS))
                if b.has(LAG_M):
                    act.wait_ge(e0_added, b.value(2, LAG_M, 2))
                if some(b.value(1, LAG_Z)):
                    act.wait_ge(x3T_done, b.value(1, LAG_Z))
                normalised(2, x3, w).then_inc(x3_ready, 1)

            def beat(b):
                if b.turn is None and b.k == LAG_M:
                    act.wait_ge(split_lo, PIECES)
                fill = 0
                if b.has(LAG_RKV):
                    if b.has(LAG_Y):
                        act.wait_ge(y_steps, b.value(Y_STEPS, LAG_Y, Y_STEPS))
                    for f in range(3):
                        to_lif(b, f, 2 * f * B, 2, None)
                    fill += 3
                if b.has(LAG_M):
                    act.wait_ge(gate_steps, b.value(GATE_STEPS, LAG_M, 7))
                    nc.scalar.activation(gexp[:], gdiff[:], ACT.Exp).then_inc(gexp_ready, 1)
                if b.has(LAG_S):
                    if b.has(LAG_Z):
                        act.wait_ge(z_ready, b.value(2, LAG_Z, 2))
                    to_lif(b, fill, COL_H2, 2, C_B2)
                    fill += 1
                if b.has(LAG_Y):
                    read_x1(b)
                elif b.has(LAG_M):
                    read_expert(b, 1)
                if b.has(LAG_M):
                    read_expert(b, 2)
                if b.has(LAG_Y):
                    if b.has(LAG_S):
                        act.wait_ge(s1_ready, b.value(FK, LAG_S, FK))
                    for f in (0, 1):
                        to_lif(b, fill + f, COL_H1 + 2 * f * B, 2, C_B1 + 2 * f)
                if b.has(LAG_M):
                    read_expert(b, 3)
                if b.has(LAG_Y):
                    to_lif(b, fill + 2, COL_H1 + 4 * B, 2, C_B1 + 4)
                if b.has(LAG_Z):
                    norm_x3(b)
                if b.has(LAG_Y):
                    to_lif(b, fill + 3, COL_H1 + 6 * B, 2, C_B1 + 6)
                if b.has(LAG_M):
                    read_expert(b, 4)
                if b.turn is None and b.k == LAG_RKV:
                    act.wait_ge(consts_loaded, 16)
                    copy(bias_stack[:], bias_raw).then_inc(bias_hi_ready, 1)
                    act.wait_ge(vec_set, 5)
                if b.has(LAG_Z):
                    act.wait_ge(x3T_done, b.value(1, LAG_Z, 1))
                    if some(b.value(E - 1, LAG_Z + 2, E - 1)):
                        act.wait_ge(expert_done, b.value(E - 1, LAG_Z + 2, E - 1))
                    copy(x3_hi[:, b.slot(LAG_Z, 2)], ps_zx[:]).then_inc(x3_hi_ready, 1)
                if b.has(LAG_M):
                    act.wait_ge(gateT_done, b.value(1, LAG_M, 1))
                    if some(b.value(1, LAG_M)):
                        act.wait_ge(bias_done, b.value(1, LAG_M))
                    copy(gate_T[:], ps_attn[0:STACK, :, 0:P]).then_inc(gateT_ready, 1)
                if b.has(LAG_X):
                    split_x(b)
                if b.turn is None and b.k == LAG_X:
                    for f in range(3):
                        act.wait_ge(wrkv_loaded[f], 16)
                        copy(wrkv_hi[:, f, :], wrkv_raw[:, f, :]).then_inc(wrkv_hi_ready, 1)
                if b.has(LAG_M):
                    for e in (5, 6, 7):
                        read_expert(b, e)
                if b.has(LAG_F):
                    act.wait_ge(fin_steps, b.value(FIN_STEPS, LAG_F, FIN_STEPS))
                    normalised(3, res, res).then_inc(res_ready, 1)
                    act.wait_ge(res_ready, b.value(1, LAG_F, 1))
                    act.dma_start(out[b.chunk(LAG_F)], res[:]).then_inc(out_stored, 16)
                if b.turn is None:
                    for p in pieces_in(b.k):
                        _, hi, _, n = pieces_of(p)
                        act.wait_ge(raw_loaded[p % RAW_SLOTS], 16 * (p // RAW_SLOTS + 1))
                        copy(hi, term[:, p % RAW_SLOTS, 0:n]).then_inc(split_hi, 1)

            run_beats(act, beat)
            act.wait_ge(out_stored, 16 * CHUNKS)

        @block.vector
        def _(dve):
            v = nc.vector

            def spikes_view(slot, tile, tiles):
                return U[:, slot, :, tile * B:(tile + tiles) * B]

            def lif_part(b, c0, c1, first_half):
                s = b.k % 2
                done = lif_half if first_half else lif
                before = 2 * STEPS * b.k if first_half else b.value(2 * STEPS, 0)

                def membrane(t):
                    if some(before + 2 * t):
                        dve.wait_ge(done, before + 2 * t)
                    v.scalar_tensor_tensor(out=U[:, s, t, c0:c1], in0=V[:, c0:c1], scalar=0.5,
                                           in1=U[:, s, t, c0:c1], op0=ALU.mult, op1=ALU.add).then_inc(done, 1)

                def reset(t):
                    dve.wait_ge(done, before + 2 * t + 1)
                    u = U[:, s, t, c0:c1]
                    v.scalar_tensor_tensor(out=V[:, c0:c1], in0=u, scalar=THRESHOLD, in1=u,
                                           op0=ALU.is_lt, op1=ALU.mult).then_inc(done, 1)

                return membrane, reset

            def after(sem_, per, lag, b, n):
                dve.wait_ge(sem_, b.value(per, lag, n))

            def plain(b):
                if b.turn is not None:
                    dve.sem_inc(dve_waited, 1)

            def z_sum(b, k):
                if k == 0:
                    if some(b.value(1, LAG_Z)):
                        dve.wait_ge(zT_done, b.value(1, LAG_Z))
                    dve.wait_ge(x1_ready, b.value(DK, LAG_Z, DK))
                s2 = U[:, (b.k - 1) % 2, :, COL_H2 + k * B:COL_H2 + (k + 1) * B]
                v.scalar_tensor_tensor(out=z[:, k, :].rearrange("p (t b) -> p t b", b=B), in0=s2,
                                       scalar=THRESHOLD,
                                       in1=x1[:, b.slot(LAG_Z, 4), k, :].rearrange("p (t b) -> p t b", b=B),
                                       op0=ALU.is_ge, op1=ALU.add).then_inc(z_ready, 1)

            def y_stage(b, step):
                slot = (b.k - 1) % 2
                chain = lambda n: after(y_steps, Y_STEPS, LAG_Y, b, n)
                if step == 0:
                    if some(b.value(1, LAG_Y)):
                        dve.wait_ge(attn_done, b.value(1, LAG_Y))
                    v.tensor_scalar(v_spikes, spikes_view(slot, 2 * DK, DK), THRESHOLD, None,
                                    ALU.is_ge).then_inc(y_steps, 1)
                if step == 1:
                    chain(1)
                    v.scalar_tensor_tensor(out=h[:], in0=spikes_view(slot, DK, DK).rearrange("p t c -> p c t"),
                                           scalar=THRESHOLD, in1=v_spikes.rearrange("p t c -> p c t"),
                                           op0=ALU.is_ge, op1=ALU.mult).then_inc(y_steps, 1)
                if step == 2:
                    chain(2)
                    v.scalar_tensor_tensor(out=h[:, :, 0], in0=h_last[:], scalar=DECAY, in1=h[:, :, 0],
                                           op0=ALU.mult, op1=ALU.add).then_inc(y_steps, 1)
                if step == 3:
                    chain(3)
                    hv = h[:].rearrange("p c t -> p (c t)")
                    v.tensor_tensor_scan(hv, decay[:].rearrange("p c t -> p (c t)"), hv, 0.0,
                                         ALU.mult, ALU.add).then_inc(y_steps, 1)
                if step == 4:
                    chain(4)
                    v.tensor_copy(h_last[:], h[:, :, STEPS - 1]).then_inc(y_steps, 1)
                    for k in range(DK):
                        v.scalar_tensor_tensor(out=y[:, k * N:(k + 1) * N].rearrange("p (t b) -> p t b", b=B),
                                               in0=spikes_view(slot, k, 1), scalar=THRESHOLD,
                                               in1=h[:, k * B:(k + 1) * B, :].rearrange("p c t -> p t c"),
                                               op0=ALU.is_ge, op1=ALU.mult).then_inc(y_steps, 1)

            def bn_stats(ln, j, src, steps):
                v.bn_stats(stats[ln][:, j, :], src).then_inc(steps, 1)

            def bn_aggr(b, ln, steps, per, lag, done):
                after(steps, per, lag, b, done)
                plain(b)
                for j in range(TILES):
                    v.bn_aggr(mv[ln][:, j, :], stats[ln][:, j, :]).then_inc(steps, 1)

            def normalise(b, ln, dst, src, steps, lag):
                dve.wait_ge(rstd_ready[ln], b.value(2, lag, 2))
                for j in range(TILES):
                    v.tensor_scalar(dst[:, j, :], src[:, j, :], mv[ln][:, j, 0:1], rstd[ln][:, j:j + 1],
                                    ALU.subtract, ALU.mult).then_inc(steps, 1)

            def mean_shift(b, ln, steps, lag):
                dve.wait_ge(rstd_ready[ln], b.value(2, lag, 2))
                v.scalar_tensor_tensor(out=shift[ln][:], in0=mv[ln][:, :, 0], scalar=-1.0, in1=rstd[ln][:],
                                       op0=ALU.mult, op1=ALU.mult).then_inc(steps, 1)

            def ln1_sum(b):
                dve.wait_ge(attn_done, b.value(1, LAG_Y, 1))
                dve.wait_ge(xa_loaded, b.value(16, LAG_Y, 16))
                if some(b.value(1, LAG_Y)):
                    dve.wait_ge(x1T_done, b.value(1, LAG_Y))
                v.tensor_tensor(x1n[:], xa[:], ps_attn[:], ALU.add).then_inc(ln1_steps, 1)

            def ln2_scale(b, j):
                if j == 0 and some(b.value(1, LAG_Z)):
                    dve.wait_ge(x3_ready, b.value(1, LAG_Z))
                v.scalar_tensor_tensor(out=w[:, j, :], in0=ps_zx[:, j, :], scalar=mv[1][:, j, 0:1],
                                       in1=ln2_gain, op0=ALU.subtract, op1=ALU.mult).then_inc(ln2_steps, 1)

            def ln2_add(b, j):
                v.scalar_tensor_tensor(out=w[:, j, :], in0=w[:, j, :], scalar=rstd[1][:, j:j + 1],
                                       in1=xb[:, j, :], op0=ALU.mult, op1=ALU.add).then_inc(ln2_steps, 1)

            def x3_low(b):
                dve.wait_ge(x3_hi_ready, b.value(1, LAG_Z, 1))
                s = b.slot(LAG_Z, 2)
                if some(b.value(E - 1, LAG_Z + 2, E - 1)):
                    dve.wait_ge(expert_done, b.value(E - 1, LAG_Z + 2, E - 1))
                v.tensor_tensor(x3_lo[:, s], ps_zx[:], x3_hi[:, s].bitcast(F32),
                                ALU.subtract).then_inc(x3_lo_ready, 1)

            def gate_stage(b, step):
                gslot = b.slot(LAG_M, 2)
                chain = lambda n: after(gate_steps, GATE_STEPS, LAG_M, b, n)
                if step == 0:
                    dve.wait_ge(e0_done, b.value(1, LAG_M, 1))
                    v.tensor_tensor(logit[:], ps_e0[:, :, D:D + E],
                                    cst[:, C_BG:C_BG + TILES * E].rearrange("p (j e) -> p j e", e=E),
                                    ALU.add).then_inc(gate_steps, 1)
                if step == 1:
                    chain(1)
                    plain(b)
                    for j in range(TILES):
                        v.max(top[:, j, :], logit[:, j, :]).then_inc(gate_steps, 1)
                if step == 2:
                    chain(3)
                    plain(b)
                    for j in range(TILES):
                        v.max_index(top_at[:, j, :], top[:, j, :], logit[:, j, :]).then_inc(gate_steps, 1)
                if step == 3:
                    chain(5)
                    v.tensor_copy(top_atf[:], top_at[:, :, 0:2]).then_inc(gate_steps, 1)
                    if some(b.value(1, LAG_M)):
                        dve.wait_ge(gexp_ready, b.value(1, LAG_M))
                    v.tensor_tensor(gdiff[:], top[:, :, 1], top[:, :, 0], ALU.subtract).then_inc(gate_steps, 1)
                if step == 4:
                    dve.wait_ge(gexp_ready, b.value(1, LAG_M, 1))
                    v.tensor_scalar(gden[:], gexp[:], 1.0, None, ALU.add).then_inc(gate_steps, 1)
                if step == 5:
                    chain(8)
                    v.reciprocal(g1st[:], gden[:]).then_inc(gate_steps, 1)
                if step == 6:
                    chain(9)
                    v.tensor_tensor(g2nd[:], gexp[:], g1st[:], ALU.mult).then_inc(gate_steps, 1)
                if step in (7, 8):
                    chain(10)
                    if step == 7:
                        if some(b.value(E - 1, LAG_M + 2, E - 1)):
                            dve.wait_ge(term_ready, b.value(E - 1, LAG_M + 2, E - 1))
                        if some(b.value(1, LAG_M + 2, 1)):
                            dve.wait_ge(gateT_done, b.value(1, LAG_M + 2, 1))
                    dst, at, weight = ((gate[:, gslot], 0, g1st), (gate_b[:], 1, g2nd))[step - 7]
                    for j in range(TILES):
                        v.tensor_scalar(dst[:, j, :], cst[:, C_IOTA:C_IOTA + E], top_atf[:, j, at:at + 1],
                                        weight[:, j:j + 1], ALU.is_equal, ALU.mult).then_inc(gate_steps, 1)
                if step == 9:
                    chain(14)
                    v.tensor_tensor(gate[:, gslot], gate[:, gslot], gate_b[:], ALU.add).then_inc(gate_steps, 1)
                if step == 10:
                    chain(GATES_DONE)
                    if some(b.value(1, LAG_M)):
                        dve.wait_ge(gateT_done, b.value(1, LAG_M))
                    for row in (ROW_HH, ROW_HL):
                        last = v.tensor_copy(gate_parts[:, :, row:row + E], gate[:, gslot])
                    last.then_inc(gate_steps, 1)
                if step == 11:
                    chain(GATES_DONE + 1)
                    v.tensor_tensor(gate_parts[:, :, ROW_LH:ROW_LH + E], gate[:, gslot],
                                    gate_parts[:, :, 0:E].bitcast(F32), ALU.subtract).then_inc(gate_steps, 1)

            def add_e0(b, j):
                if j == 0:
                    dve.wait_ge(gate_steps, b.value(GATE_STEPS, LAG_M, GATES_DONE))
                    if some(b.value(SUM_STEPS, LAG_M + 1)):
                        dve.wait_ge(sum_steps, b.value(SUM_STEPS, LAG_M + 1))
                v.scalar_tensor_tensor(out=acc[:, b.slot(LAG_M, 2), j, :], in0=ps_e0[:, j, 0:D],
                                       scalar=gate[:, b.slot(LAG_M, 2), j, 0:1], in1=x3[:, j, :],
                                       op0=ALU.mult, op1=ALU.add).then_inc(e0_added, 1)

            def fin_stage(b, step):
                chain = lambda n: after(fin_steps, FIN_STEPS, LAG_F, b, n)
                if step == 0:
                    dve.wait_ge(bias_done, b.value(1, LAG_F, 1))
                    dve.wait_ge(e0_added, b.value(2, LAG_F, 2))
                    v.tensor_tensor(acc[:, b.slot(LAG_F, 2)], acc[:, b.slot(LAG_F, 2)], ps_zx[:], ALU.add).then_inc(fin_steps, 1)
                if step == 1:
                    dve.wait_ge(sum_steps, b.value(SUM_STEPS, LAG_F, SUM_STEPS))
                    for j in range(TILES):
                        bn_stats(3, j, res[:, j, :], fin_steps)
                if step == 2:
                    bn_aggr(b, 3, fin_steps, FIN_STEPS, LAG_F, 3)
                if step == 3:
                    mean_shift(b, 3, fin_steps, LAG_F)

            def side(b, slot):
                at = STEADY if not b.edge else FILL if b.k < FIRST_STEADY else DRAIN
                if b.has(LAG_Z):
                    if slot == at["z_sum"]:
                        z_sum(b, 0)
                        z_sum(b, 1)
                if b.has(LAG_Y):
                    for step in range(5):
                        if slot == at["y"][step]:
                            y_stage(b, step)
                if b.has(LAG_S) and b.dve_spikes and slot == at["spikes_h1"]:
                    spikes_h1(b)
                if b.has(LAG_F) and slot == at["fin_sum"]:
                    fin_stage(b, 0)
                if b.has(LAG_Z):
                    for j in range(TILES):
                        if slot == at["ln2_stats"][j]:
                            if j == 0:
                                dve.wait_ge(zT_done, b.value(1, LAG_Z, 1))
                            bn_stats(1, j, ps_zx[:, j, :], ln2_steps)
                    if slot == at["ln2_aggr"]:
                        bn_aggr(b, 1, ln2_steps, LN2_STEPS, LAG_Z, 2)
                if b.has(LAG_Y):
                    if slot == at["ln1_sum"]:
                        ln1_sum(b)
                    for j in range(TILES):
                        if slot == at["ln1_stats"][j]:
                            if j == 0:
                                after(ln1_steps, LN1_STEPS, LAG_Y, b, 1)
                            bn_stats(0, j, x1n[:, j, :], ln1_steps)
                    if slot == at["ln1_aggr"]:
                        bn_aggr(b, 0, ln1_steps, LN1_STEPS, LAG_Y, 3)
                    if slot == at["ln1_norm"]:
                        normalise(b, 0, x1n, x1n, ln1_steps, LAG_Y)
                if b.has(LAG_M):
                    for step in range(12):
                        if slot == at["gate"][step]:
                            gate_stage(b, step)
                if b.has(LAG_Z):
                    for j in range(TILES):
                        if slot == at["ln2_scale"][j]:
                            if j == 0:
                                after(ln2_steps, LN2_STEPS, LAG_Z, b, 4)
                            ln2_scale(b, j)
                    if slot == at["ln2_add"]:
                        after(ln2_steps, LN2_STEPS, LAG_Z, b, 6)
                        dve.wait_ge(rstd_ready[1], b.value(2, LAG_Z, 2))
                        dve.wait_ge(xb_ready, b.value(1, LAG_Z, 1))
                        ln2_add(b, 0)
                        ln2_add(b, 1)
                    if slot == at["ln3_stats"]:
                        after(ln2_steps, LN2_STEPS, LAG_Z, b, 8)
                        bn_stats(2, 0, w[:, 0, :], ln3_steps)
                        bn_stats(2, 1, w[:, 1, :], ln3_steps)
                    if slot == at["ln3_aggr"]:
                        bn_aggr(b, 2, ln3_steps, LN3_STEPS, LAG_Z, 2)
                if b.has(LAG_M):
                    for j in range(TILES):
                        if slot == at["add_e0"][j]:
                            add_e0(b, j)
                if b.has(LAG_Z) and slot == at["ln3_shift"]:
                    mean_shift(b, 2, ln3_steps, LAG_Z)
                if b.has(LAG_F):
                    if slot == at["fin_stats"]:
                        fin_stage(b, 1)
                    if slot == at["fin_aggr"]:
                        fin_stage(b, 2)
                if b.has(LAG_Z) and slot == at["x3_low"]:
                    x3_low(b)
                if b.has(LAG_F) and slot == at["fin_shift"]:
                    fin_stage(b, 3)

            def lif_columns(b):
                if b.turn is not None:
                    return 0, COLS
                has = [0 <= b.k - lag < CHUNKS for lag in (0, 2, 4)]
                edges = [0, COL_H1, COL_H2, COLS]
                return edges[has.index(True)], edges[3 - has[::-1].index(True)]

            def spikes_h1(b):
                if some(b.w2_fills()):
                    dve.wait_ge(proj_filled, b.w2_fills())
                for ft in range(FK - b.dve_spikes, FK):
                    v.tensor_scalar(s1[:, ft, :].rearrange("p (t b) -> p t b", b=B),
                                    U[:, (b.k - 1) % 2, :, COL_H1 + ft * B:COL_H1 + (ft + 1) * B],
                                    THRESHOLD, None, ALU.is_ge).then_inc(s1_ready, 1)

            def beat(b):
                if 0 < b.k <= LIF_BEATS:
                    dve.wait_ge(lif, b.value(2 * STEPS, 0))
                side(b, -1)
                if b.lif():
                    c0, c1 = lif_columns(b)
                    if some(b.fills()):
                        dve.wait_ge(proj_read, b.fills())
                    mid = (c0 + c1) // 2 if b.halves else c0
                    membrane, reset = lif_part(b, mid, c1, False)
                    if b.halves:
                        membrane_half, reset_half = lif_part(b, c0, mid, True)
                    for t in range(STEPS):
                        if b.halves:
                            membrane_half(t)
                        membrane(t)
                        side(b, 2 * t)
                        if b.halves:
                            reset_half(t)
                        reset(t)
                        side(b, 2 * t + 1)
                else:
                    for slot in range(2 * STEPS):
                        side(b, slot)

            v.memset(V[:], 0.0).then_inc(vec_set, 1)
            v.memset(h_last[:], 0.0).then_inc(vec_set, 1)
            v.memset(decay[:], DECAY).then_inc(vec_set, 1)
            v.memset(gate_parts[:].bitcast(F32), 0.0).then_inc(vec_set, 1)
            dve.wait_ge(vec_set, 4)
            v.memset(decay[:, :, 0], 0.0).then_inc(vec_set, 1)
            for f in range(3):
                dve.wait_ge(wrkv_hi_ready, f + 1)
                v.tensor_tensor(wrkv_lo[:, f, :], wrkv_raw[:, f, :], wrkv_hi[:, f, :].bitcast(F32),
                                ALU.subtract).then_inc(wrkv_lo_ready, 1)
            dve.wait_ge(vec_set, 5)
            dve.wait_ge(bias_hi_ready, 1)
            rows = slice(ROW_HL, STACK)
            v.tensor_tensor(bias_stack[rows, :], bias_raw[rows, :], bias_stack[rows, :].bitcast(F32),
                            ALU.subtract).then_inc(bias_lo_ready, 1)
            run_beats(dve, beat)

        @block.gpsimd
        def _(pool):
            g = nc.gpsimd

            def plain(b):
                if b.turn is not None:
                    pool.sem_inc(pool_waited, 1)

            def reciprocal_std(b, ln, steps, per, lag, done):
                pool.wait_ge(steps, b.value(per, lag, done))
                plain(b)
                g.tensor_scalar(veps[ln][:], mv[ln][:, :, 1], EPS, None, ALU.add).then_inc(rstd_ready[ln], 1)
                pool.wait_ge(rstd_ready[ln], b.value(2, lag, 1))
                g.tensor_tensor(rstd[ln][:], veps[ln][:], neg_half[:], ALU.pow).then_inc(rstd_ready[ln], 1)

            def spikes_h1(b, part):
                if part == 0:
                    if some(b.value(2 * STEPS, 0)):
                        pool.wait_ge(lif, b.value(2 * STEPS, 0))
                    if some(b.w2_fills()):
                        pool.wait_ge(proj_filled, b.w2_fills())
                    plain(b)
                for e in range(2):
                    ft = 2 * part + e
                    last = g.tensor_scalar(s1[:, ft, :].rearrange("p (t b) -> p t b", b=B),
                                           U[:, (b.k - 1) % 2, :, COL_H1 + ft * B:COL_H1 + (ft + 1) * B],
                                           THRESHOLD, None, ALU.is_ge)
                last.then_inc(s1_ready, 2)

            def split_x(b):
                pool.wait_ge(x_hi_ready, b.value(1, LAG_X, 1))
                g.tensor_tensor(x_lo[:], xt[:, b.slot(LAG_X, 2)], x_hi[:].bitcast(F32),
                                ALU.subtract).then_inc(x_lo_ready, 1)

            def add_term(b, lag, e):
                pool.wait_ge(term_ready, b.value(E - 1, lag, e))
                if e == 2:
                    if some(b.value(SUM_STEPS, lag)):
                        pool.wait_ge(sum_steps, b.value(SUM_STEPS, lag))
                    first = term[:, 0, 0:PIECE]
                else:
                    pool.wait_ge(sum_steps, b.value(SUM_STEPS, lag, e - 2))
                    first = psum_terms[:].rearrange("p j d -> p (j d)")
                g.tensor_tensor(psum_terms[:].rearrange("p j d -> p (j d)"), first,
                                term[:, (e - 1) % RAW_SLOTS, 0:PIECE], ALU.add).then_inc(sum_steps, 1)

            def add_all(b):
                pool.wait_ge(sum_steps, b.value(SUM_STEPS, LAG_F, SUM_STEPS - 1))
                pool.wait_ge(fin_steps, b.value(FIN_STEPS, LAG_F, 1))
                if some(b.value(16, LAG_F)):
                    pool.wait_ge(out_stored, b.value(16, LAG_F))
                g.tensor_tensor(res[:], acc[:, b.slot(LAG_F, 2)], psum_terms[:], ALU.add).then_inc(sum_steps, 1)

            def add_bias(b):
                if b.turn is None:
                    pool.wait_ge(consts_loaded, 16)
                pool.wait_ge(xb_loaded, b.value(16, LAG_Z, 16))
                for j in range(TILES):
                    last = g.tensor_tensor(xb[:, j, :], xb[:, j, :], ln2_bias, ALU.add)
                last.then_inc(xb_ready, 1)

            def split_x1(b):
                for k in range(DK):
                    pool.wait_ge(x1_ready, b.value(DK, LAG_Y, k + 1))
                    g.tensor_tensor(x1_lo[:, k, :], x1[:, b.slot(LAG_Y, 4), k, :], x1_hi[:, k, :].bitcast(F32),
                                    ALU.subtract).then_inc(x1_lo_ready, 1)

            def beat(b):
                has_y, has_z, has_m, has_f = (b.has(lag) for lag in (LAG_Y, LAG_Z, LAG_M, LAG_F))
                if b.has(LAG_S):
                    for part in range((FK - b.dve_spikes) // 2):
                        spikes_h1(b, part)
                if b.edge:
                    if has_z:
                        add_bias(b)
                    if has_f:
                        for e in (4, 5, 6, 7):
                            add_term(b, LAG_F, e)
                else:
                    add_bias(b)
                    add_term(b, LAG_F, 4)
                if has_y:
                    reciprocal_std(b, 0, ln1_steps, LN1_STEPS, LAG_Y, 5)
                if has_z:
                    reciprocal_std(b, 1, ln2_steps, LN2_STEPS, LAG_Z, 4)
                if b.edge:
                    if has_y:
                        split_x1(b)
                    if has_f:
                        add_all(b)
                else:
                    add_term(b, LAG_F, 5)
                    add_term(b, LAG_F, 6)
                    split_x1(b)
                    add_term(b, LAG_F, 7)
                    add_all(b)
                if has_z:
                    reciprocal_std(b, 2, ln3_steps, LN3_STEPS, LAG_Z, 4)
                if not b.edge:
                    add_term(b, LAG_M, 2)
                if has_f:
                    reciprocal_std(b, 3, fin_steps, FIN_STEPS, LAG_F, 5)
                if has_m:
                    if b.edge:
                        add_term(b, LAG_M, 2)
                    add_term(b, LAG_M, 3)
                if b.has(LAG_X):
                    split_x(b)
                if b.turn is None:
                    for p in pieces_in(b.k):
                        _, hi, lo, n = pieces_of(p)
                        pool.wait_ge(split_hi, p + 1)
                        g.tensor_tensor(lo, term[:, p % RAW_SLOTS, 0:n], hi.bitcast(F32),
                                        ALU.subtract).then_inc(split_lo, 1)

            g.memset(neg_half[:], -0.5).then_inc(pool_set, 1)
            pool.wait_ge(pool_set, 1)
            run_beats(pool, beat)


def kernel(**inputs):
    import numpy as np
    import concourse.bacc as bacc
    from concourse.bass_utils import run_bass_kernel_spmd

    a = {k: np.asarray(v) for k, v in inputs.items()}
    x = a["L0_attn_x"]
    by_time = x.transpose(1, 0, 2).reshape(CHUNKS, N, D)
    col = lambda v, n: v.reshape(n, P).T
    wide = lambda v: np.broadcast_to(v.reshape(1, -1), (P, v.size))
    k_first = lambda m: m.reshape(m.shape[0] // P, P, m.shape[1]).transpose(1, 0, 2)
    we = a["L0_ffn_We"]
    bias_rows = np.zeros((P, D), np.float32)
    for row in (ROW_HH, ROW_LH, ROW_HL):
        bias_rows[row:row + E] = a["L0_ffn_be"]
    consts = np.concatenate([
        col(a["L0_attn_b1"], FK), col(a["L0_attn_b2"], DK), col(a["L0_attn_ln1_g"], DK),
        col(a["L0_attn_ln1_b"], DK), wide(a["L0_ffn_bg"]), wide(a["L0_ffn_bg"]),
        wide(np.arange(E, dtype=np.float32)), np.eye(P, dtype=np.float32),
        wide(a["L0_attn_ln2_g"]), wide(a["L0_attn_ln2_b"]), bias_rows], axis=1)
    arrays = {
        "x_T": np.concatenate([by_time.transpose(0, 2, 1).reshape(CHUNKS, DK, P, N).transpose(0, 2, 1, 3),
                               np.zeros((1, P, DK, N), np.float32)]),
        "x_tok": by_time.reshape(CHUNKS, TILES, P, D).transpose(0, 2, 1, 3),
        "w_rkv": np.stack([k_first(a[f"L0_attn_W{m}"].T).reshape(P, DK * D) for m in "rkv"]),
        "w_o": k_first(a["L0_attn_Wo"].T),
        "w_1": k_first(a["L0_attn_W1"].T).reshape(P, DK * F),
        "w_2": k_first(a["L0_attn_W2"].T).reshape(P, FK * D),
        "w_e0": k_first(np.concatenate([we[0], a["L0_ffn_Wg"]], axis=1)).reshape(P, PIECE0),
        "w_e": np.stack([k_first(we[e]).reshape(P, PIECE) for e in range(1, E)]),
        "consts": consts,
    }
    nc = bacc.Bacc("TRN2", target_bir_lowering=False, num_devices=1)
    args = []
    for name in arrays:
        arrays[name] = np.ascontiguousarray(arrays[name])
        args.append(nc.dram_tensor(name, arrays[name].shape, F32, kind="ExternalInput").ap())
    out = nc.dram_tensor("out", (CHUNKS, P, TILES, D), F32, kind="ExternalOutput").ap()
    build(nc, *args, out)
    r = run_bass_kernel_spmd(nc, [arrays], core_ids=[0])
    got = np.asarray(r.results[0]["out"])
    return got.transpose(0, 2, 1, 3).reshape(T, B, D).transpose(1, 0, 2)
```
